# Optimizing a Trainium2 kernel written in Bass

```python
import numpy as np
import jax
import jax.numpy as jnp

def _softmax(x, axis=-1):
    return jax.nn.softmax(x, axis=axis)

def _gelu(x):
    return jax.nn.gelu(x, approximate=True)

def _silu(x):
    return jax.nn.silu(x)

def _sigmoid(x):
    return jax.nn.sigmoid(x)

def _layernorm(x, axis=-1, eps=1e-05):
    m = jnp.mean(x, axis=axis, keepdims=True)
    v = jnp.var(x, axis=axis, keepdims=True)
    return (x - m) / jnp.sqrt(v + eps)

def _scatter_add(tgt, idx, src, axis=0):
    return tgt.at[idx].add(src)

def _segment_sum(src, seg, n):
    return jax.ops.segment_sum(src, seg, n)
kernel_name = 'mk_adj_resnorm_d2_adj_r2_678535'

def setup_inputs(seed: int=0):
    np.random.seed(seed)
    _w = jnp.asarray

    def _rec_inputs():
        import jax
        import jax.numpy as jnp
        _gk = jax.random.key(seed)
        x = -9.229e-05 + 0.9999 * jax.random.normal(jax.random.fold_in(_gk, 1), (128, 64, 512), jnp.float32)
        _a = jax.random.bernoulli(jax.random.fold_in(_gk, 2), 0.0625, (64, 64))
        _a = jnp.logical_or(_a, jnp.swapaxes(_a, -1, -2))
        _a = jnp.logical_or(_a, jnp.eye(64, dtype=bool))
        _af = _a.astype(jnp.float32)
        adj = _af
        return (x, adj)
    x, adj = _rec_inputs()

    def _L0_gnn_setup():
        import jax, jax.numpy as jnp
        import numpy as np
        DIM = 199
        K_HOP = 3

        def _khop_support(n, k):
            A = np.eye(n, dtype=np.float64)
            idx = np.arange(n)
            A[idx, (idx + 1) % n] = 1.0
            A[(idx + 1) % n, idx] = 1.0
            S = np.linalg.matrix_power(A, k)
            return (S > 0).astype(np.float32)
        key = jax.random.key(seed)
        kx, kk = jax.random.split(key)
        batch, n, f = (128, DIM, 512)
        x = jax.random.normal(kx, (batch, n, f), dtype=jnp.float32)
        support = jnp.asarray(_khop_support(n, K_HOP))
        limit = float(np.sqrt(6.0 / (n + n)))
        kernel = jax.random.uniform(kk, (n, n), minval=-limit, maxval=limit, dtype=jnp.float32)
        bias = jnp.zeros((f,), dtype=jnp.float32)
        return {'x': x, 'support': support, 'kernel': kernel, 'bias': bias}
    _L0_gnn_all = _L0_gnn_setup()
    _L0_gnn_in = {k: v for k, v in _L0_gnn_all.items() if k in ('bias',)}
    del _L0_gnn_all

    def _L1_gnn_setup():
        import jax, jax.numpy as jnp
        import numpy as np
        EPS = 1e-08

        def _row_stochastic_causal(A, causal_mask):
            A = A * causal_mask
            deg = jnp.maximum(A.sum(axis=-1, keepdims=True), EPS)
            return A / deg
        key = jax.random.key(seed)
        k = jax.random.split(key, 5)
        B, N, D = (4, 1024, 512)
        s = 1.0 / np.sqrt(D)
        h = jax.random.normal(k[0], (B, N, D), dtype=jnp.float32)
        W_lang = jax.random.normal(k[1], (D, D), dtype=jnp.float32) * s
        W_grav = jax.random.normal(k[2], (D, D), dtype=jnp.float32) * s
        W_V = jax.random.normal(k[3], (D, D), dtype=jnp.float32) * s
        W_O = jax.random.normal(k[4], (D, D), dtype=jnp.float32) * s
        causal_mask = jnp.tril(jnp.ones((N, N), dtype=jnp.float32))
        gate_logit = jnp.zeros((), jnp.float32)
        log_sigma = jnp.zeros((), jnp.float32)
        return {'h': h, 'causal_mask': causal_mask, 'W_lang': W_lang, 'W_grav': W_grav, 'W_V': W_V, 'W_O': W_O, 'gate_logit': gate_logit, 'log_sigma': log_sigma}
    _L1_gnn_all = _L1_gnn_setup()
    _L1_gnn_in = {k: v for k, v in _L1_gnn_all.items() if k in ('W_lang', 'W_grav', 'W_V', 'W_O', 'gate_logit', 'log_sigma')}
    del _L1_gnn_all
    return {'x': x, 'adj': adj, 'L0_gnn_bias': _L0_gnn_in['bias'], 'L1_gnn_W_lang': _L1_gnn_in['W_lang'], 'L1_gnn_W_grav': _L1_gnn_in['W_grav'], 'L1_gnn_W_V': _L1_gnn_in['W_V'], 'L1_gnn_W_O': _L1_gnn_in['W_O'], 'L1_gnn_gate_logit': _L1_gnn_in['gate_logit'], 'L1_gnn_log_sigma': _L1_gnn_in['log_sigma']}

def reference(x, adj, L0_gnn_bias, L1_gnn_W_lang, L1_gnn_W_grav, L1_gnn_W_V, L1_gnn_W_O, L1_gnn_gate_logit, L1_gnn_log_sigma):
    import jax
    import jax.numpy as jnp

    def _L0_gnn_ref(x, support, kernel, bias):
        import jax, jax.numpy as jnp
        import numpy as np
        DIM = 199
        K_HOP = 3

        def _khop_support(n, k):
            A = np.eye(n, dtype=np.float64)
            idx = np.arange(n)
            A[idx, (idx + 1) % n] = 1.0
            A[(idx + 1) % n, idx] = 1.0
            S = np.linalg.matrix_power(A, k)
            return (S > 0).astype(np.float32)
        W = support * kernel
        out = jnp.einsum('bnf,nm->bmf', x, W)
        out = out + bias
        return out

    def _L1_gnn_ref(h, causal_mask, W_lang, W_grav, W_V, W_O, gate_logit, log_sigma):
        import jax, jax.numpy as jnp
        import numpy as np
        EPS = 1e-08

        def _row_stochastic_causal(A, causal_mask):
            A = A * causal_mask
            deg = jnp.maximum(A.sum(axis=-1, keepdims=True), EPS)
            return A / deg
        z_l = jnp.einsum('bnd,ed->bne', h, W_lang)
        z_g = jnp.einsum('bnd,ed->bne', h, W_grav)
        v = jnp.einsum('bnd,ed->bne', h, W_V)
        N = h.shape[-2]
        not_eye = 1.0 - jnp.eye(N, dtype=h.dtype)
        zn = z_l / jnp.maximum(jnp.linalg.norm(z_l, axis=-1, keepdims=True), EPS)
        A_l = jnp.maximum(jnp.einsum('bnd,bmd->bnm', zn, zn), 0.0) * not_eye
        sq = jnp.sum(z_g * z_g, axis=-1, keepdims=True)
        d2 = jnp.maximum(sq + jnp.swapaxes(sq, -1, -2) - 2.0 * jnp.einsum('bnd,bmd->bnm', z_g, z_g), 0.0)
        sigma = jnp.exp(log_sigma)
        A_g = jnp.exp(-d2 / (2.0 * sigma * sigma)) * not_eye
        K_l = _row_stochastic_causal(A_l, causal_mask)
        K_g = _row_stochastic_causal(A_g, causal_mask)
        w_l = jax.nn.sigmoid(gate_logit)
        K = w_l * K_l + (1.0 - w_l) * K_g
        out = jnp.einsum('bnm,bmd->bnd', K, v)
        return jnp.einsum('bnd,ed->bne', out, W_O)
    x = _layernorm(x + _L0_gnn_ref(x, adj, adj, L0_gnn_bias), axis=-1)
    x = _layernorm(x + _L1_gnn_ref(x, adj, L1_gnn_W_lang, L1_gnn_W_grav, L1_gnn_W_V, L1_gnn_W_O, L1_gnn_gate_logit, L1_gnn_log_sigma), axis=-1)
    return x

_drawn_inputs = setup_inputs


def setup_inputs(seed=0):
    import zlib

    import numpy as np

    out = dict(_drawn_inputs(seed))
    spreads = {'L0_gnn_bias': (0.0, 0.1)}
    factors = {}
    for name, (base, spread) in spreads.items():
        noise = np.random.default_rng([zlib.crc32(name.encode()), seed]).standard_normal(out[name].shape)
        drawn = base * np.exp(spread * noise) if base else spread * noise
        out[name] = jnp.asarray(drawn.astype(out[name].dtype))
    for name, factor in factors.items():
        out[name] = (out[name] * factor).astype(out[name].dtype)
    return out
```

```python
import concourse.bass as bass
from concourse import mybir
from contextlib import ExitStack


def bass_two_layer_graph_resnorm(
    nc: bass.Bass,
    x: bass.AP,
    adj: bass.AP,
    bias: bass.AP,
    w_lang: bass.AP,
    w_grav: bass.AP,
    w_v: bass.AP,
    w_o: bass.AP,
    gate_logit: bass.AP,
    log_sigma: bass.AP,
    out: bass.AP,
):
    fp32 = mybir.dt.float32
    fp32r = mybir.dt.float32r
    ALU = mybir.AluOpType
    ACT = mybir.ActivationFunctionType

    B, N, D = x.shape
    R = 128
    NP = 4
    NG = B * N // (R * NP)
    DC = D // R
    GT = NP * R
    LN_EPS = 1e-5
    EPS = 1e-8
    L, G = 0, 1
    NBLK = DC * (DC + 1) // 2
    ROW_AT = [i * DC - i * (i - 1) // 2 for i in range(DC)]
    PROJ = [(L, 3), (L, 0), (L, 2), (L, 1), (G, 3), (G, 0), (G, 2), (G, 1)] + [("u", p) for p in range(NP)]
    NPROJ = len(PROJ)
    NRING = 3
    NSETUP = 2 * DC + 2 * DC
    assert NG % 2 == 0 and NPROJ % NRING == 0

    x_v = x.rearrange("(g p b) n f -> g (b n) p f", p=NP, b=2)
    out_v = out.rearrange("(g p b) n f -> g (b n) p f", p=NP, b=2)

    ctx = ExitStack()
    with ctx:
        def sb(name, shape, dt=fp32):
            return ctx.enter_context(nc.sbuf_tensor(name, shape, dt))

        def pb(name):
            return ctx.enter_context(nc.psum_tensor(name, [R, 512], fp32))

        def sem(name):
            return ctx.enter_context(nc.semaphore(name))

        ident = sb("ident", [R, R])
        off_diag = sb("off_diag", [R, R])
        adj_bd = sb("adj_bd", [R, R])
        mask = sb("mask", [R, R])
        mix = sb("mix", [R, R])
        mix_hi = sb("mix_hi", [R, R], fp32r)
        mix_lo = sb("mix_lo", [R, R], fp32r)
        bias_bc = sb("bias_bc", [R, D])
        gates = sb("gates", [R, 2])
        gate_e = sb("gate_e", [R, 2])
        gate_t = sb("gate_t", [R, 4])
        neg_inv = sb("neg_inv", [R, 1])
        mixw = sb("mixw", [R, 4])
        pow_half = sb("pow_half", [R, 4])
        T_hi = [sb(f"T_hi{s}", [R, NBLK, R], fp32r) for s in (L, G)]
        T_lo = [sb(f"T_lo{s}", [R, NBLK, R], fp32r) for s in (L, G)]
        M_hi = sb("M_hi", [R, DC, D], fp32r)
        M_lo = sb("M_lo", [R, DC, D], fp32r)
        x_sb = sb("x_sb", [R, NP, D])
        x_hi = sb("x_hi", [R, NP, D], fp32r)
        x_lo = sb("x_lo", [R, NP, D], fp32r)
        y_sb = sb("y_sb", [R, 2, D])
        h_sb = [sb(f"h_sb{i}", [R, NP, D]) for i in range(2)]
        hT_hi = [sb(f"hT_hi{i}", [R, DC, GT], fp32r) for i in range(2)]
        hT_lo = [sb(f"hT_lo{i}", [R, DC, GT], fp32r) for i in range(2)]
        yT_hi = sb("yT_hi", [R, DC, 2, GT], fp32r)
        yT_lo = sb("yT_lo", [R, DC, 2, GT], fp32r)
        u_hi = sb("u_hi", [R, NP, D], fp32r)
        u_lo = sb("u_lo", [R, NP, D], fp32r)
        P_sb = [sb(f"P_sb{q}", [R, 2, 2, R]) for q in range(2)]
        diag_scr = sb("diag_scr", [R, 4, R])
        S2 = sb("S2", [R, 2, 2, R])
        X0 = sb("X0", [R, 2, R])
        X_l = sb("X_l", [R, 2, R])
        negd = sb("negd", [R, 2, R])
        E_g = sb("E_g", [R, 2, R])
        X_g = sb("X_g", [R, 2, R])
        K_l = sb("K_l", [R, 2, R])
        K_sb = sb("K_sb", [R, 2, R])
        KT_hi = sb("KT_hi", [R, 2, R], fp32r)
        KT_lo = sb("KT_lo", [R, 2, R], fp32r)
        sq = [sb(f"sq{q}", [R, 2, 2]) for q in range(2)]
        sq_floor = [sb(f"sq_floor{q}", [R, 2, 2]) for q in range(2)]
        norms = [sb(f"norms{q}", [R, 2, 2]) for q in range(2)]
        exp_bias = [sb(f"exp_bias{q}", [R, 2]) for q in range(2)]
        floors = [sb(f"floors{q}", [R, 4]) for q in range(2)]
        sums = sb("sums", [R, 4])
        dens = sb("dens", [R, 4])
        recs = sb("recs", [R, 4])
        coef = sb("coef", [R, 4])
        y_bn = sb("y_bn", [R, NP, 6])
        y_mv = sb("y_mv", [R, NP, 2])
        y_ve = sb("y_ve", [R, NP])
        y_rs = sb("y_rs", [R, NP])
        y_nb = sb("y_nb", [R, NP])
        z_bn = sb("z_bn", [R, NP, 6])
        z_mv = sb("z_mv", [R, NP, 2])
        z_ve = sb("z_ve", [R, NP])
        z_rs = sb("z_rs", [R, NP])
        z_nb = sb("z_nb", [R, NP])
        z_sb = sb("z_sb", [R, 2, D])
        o_sb = sb("o_sb", [R, NP, D])
        w_raw = [sb("w_raw", [R, DC, D]), o_sb, h_sb[1]]
        yT_w = [t[:, :, :, :].rearrange("p a s t -> p (a s t)") for t in (yT_hi, yT_lo)]

        def half(view, k):
            return view[:, k * DC * D:(k + 1) * DC * D].rearrange("p (c d) -> p c d", c=DC)

        W_hi = [half(yT_w[0], 0), half(yT_w[0], 1), u_hi[:, :, :], hT_hi[1][:, :, :]]
        W_lo = [half(yT_w[1], 0), half(yT_w[1], 1), u_lo[:, :, :], hT_lo[1][:, :, :]]

        ring = [pb(f"ring{i}") for i in range(NRING)]
        bank_x = pb("bank_x")
        bank_k = pb("bank_k")
        bank_p = pb("bank_p")
        bank_pt = pb("bank_pt")
        bank_r = pb("bank_r")
        p_ps = bank_p[:, :].rearrange("r (p s c) -> r p s c", p=2, s=2)
        pt_ps = bank_pt[:, :].rearrange("r (p s c) -> r p s c", p=2, s=2)
        row_ps = bank_r[:, :].rearrange("r (s p c) -> r s p c", p=2, s=2)
        kt_ps = bank_pt[:, 0:2 * R].rearrange("r (p c) -> r p c", p=2)

        w_loaded = [sem(f"w_loaded{i}") for i in range(4)]
        adj_zeroed = sem("adj_zeroed")
        adj_loaded = sem("adj_loaded")
        bias_loaded = sem("bias_loaded")
        gates_loaded = sem("gates_loaded")
        ident_ready = sem("ident_ready")
        pow_ready = sem("pow_ready")
        mix_steps = sem("mix_steps")
        gate_exp = sem("gate_exp")
        gate_steps = sem("gate_steps")
        w_hi_done = sem("w_hi_done")
        w_lo_done = sem("w_lo_done")
        setup_done = sem("setup_done")
        setup_hi = sem("setup_hi")
        setup_split = sem("setup_split")
        x_loaded = sem("x_loaded")
        x_hi_done = sem("x_hi_done")
        x_lo_done = sem("x_lo_done")
        l0_done = sem("l0_done")
        y_added = sem("y_added")
        y_counted = sem("y_counted")
        y_stats = sem("y_stats")
        y_ve_done = sem("y_ve_done")
        y_rs_done = sem("y_rs_done")
        y_scale = sem("y_scale")
        h_ready = sem("h_ready")
        hT_done = sem("hT_done")
        hT_hi_done = sem("hT_hi_done")
        hT_split = sem("hT_split")
        proj_done = sem("proj_done")
        proj_hi = sem("proj_hi")
        proj_split = sem("proj_split")
        gram_done = sem("gram_done")
        p_copied = sem("p_copied")
        sq_done = sem("sq_done")
        floor_done = sem("floor_done")
        norm_done = sem("norm_done")
        cols_ready = sem("cols_ready")
        pt_done = sem("pt_done")
        rows_done = sem("rows_done")
        s2_done = sem("s2_done")
        x0_done = sem("x0_done")
        xl_done = sem("xl_done")
        negd_done = sem("negd_done")
        exp_done = sem("exp_done")
        xg_done = sem("xg_done")
        dens_done = sem("dens_done")
        recs_done = sem("recs_done")
        coef_done = sem("coef_done")
        kl_done = sem("kl_done")
        k_done = sem("k_done")
        kt_done = sem("kt_done")
        kt_hi_done = sem("kt_hi_done")
        kt_split = sem("kt_split")
        ku_done = sem("ku_done")
        z_added = sem("z_added")
        z_counted = sem("z_counted")
        z_stats = sem("z_stats")
        z_ve_done = sem("z_ve_done")
        z_rs_done = sem("z_rs_done")
        z_scale = sem("z_scale")
        o_ready = sem("o_ready")
        stored = [sem(f"stored{p}") for p in range(NP)]

        block = ctx.enter_context(nc.Block())

        def parts(hi, lo, hi2, lo2):
            return [(hi, hi2), (hi, lo2), (lo, hi2)]

        def settle(engine):
            engine.nop(nofuse=True)

        @block.sync
        def _(sp):
            sp.wait_ge(adj_zeroed, 1)
            for b in range(2):
                s = slice(b * N, (b + 1) * N)
                sp.dma_start(adj_bd[s, s], adj).then_inc(adj_loaded, 16)
            sp.dma_start(x_sb[:, :, :], x_v[0]).then_inc(x_loaded, 16)
            for i, w in enumerate((w_lang, w_grav, w_v)):
                sp.dma_start(w_raw[i][:, :, :], w.rearrange("(c p) d -> p c d", p=R)).then_inc(w_loaded[i], 16)
            sp.dma_start(bias_bc[:, :], bias.partition_broadcast(R)).then_inc(bias_loaded, 16)
            sp.dma_start(gates[:, 0:1], gate_logit.partition_broadcast(R)).then_inc(gates_loaded, 16)
            sp.dma_start(gates[:, 1:2], log_sigma.partition_broadcast(R)).then_inc(gates_loaded, 16)
            sp.wait_ge(x_lo_done, NP)
            sp.dma_start(x_sb[:, :, :], x_v[1]).then_inc(x_loaded, 16)
            sp.wait_ge(w_lo_done, 1)
            sp.dma_start(w_raw[0][:, :, :], w_o.rearrange("(c p) d -> p c d", p=R)).then_inc(w_loaded[3], 16)

            def load(g):
                sp.wait_ge(x_lo_done, NP * g)
                sp.dma_start(x_sb[:, :, :], x_v[g]).then_inc(x_loaded, 16)

            def store(g):
                for p in range(NP):
                    sp.wait_ge(o_ready, NP * g + p + 1)
                    sp.dma_start(out_v[g][:, p, :], o_sb[:, p, :]).then_inc(stored[p], 16)

            load(2)
            with sp.Fori(1, NG - 2, 1) as g:
                store(g - 1)
                load(g + 2)
            store(NG - 3)
            store(NG - 2)
            store(NG - 1)
            for p in range(NP):
                sp.wait_ge(stored[p], 16 * NG)

        @block.tensor
        def _(pe):
            def layer0(g, p):
                pe.wait_ge(x_lo_done, NP * g + p + 1)
                if p:
                    pe.wait_ge(y_added, NP * g + p)
                for n, (w, r) in enumerate(parts(mix_hi, mix_lo, x_hi, x_lo)):
                    last = pe.matmul(bank_x[:, :], w[:, :], r[:, p, :], start=n == 0, stop=n == 2)
                last.then_inc(l0_done, 1)

            def transpose_h(g, par, p):
                pe.wait_ge(h_ready, NP * g + p + 1)
                if p >= 2:
                    pe.wait_ge(hT_split, NP * g + p - 1)
                elif p == 0:
                    pe.wait_ge(y_added, NP * g + NP)
                bank = (bank_x, bank_k)[p % 2]
                for c in range(DC):
                    last = pe.transpose(bank[:, c * R:(c + 1) * R], h_sb[par][:, p, c * R:(c + 1) * R], ident[:, :])
                last.then_inc(hT_done, 1)

            def project(g, par, k):
                kind, j = PROJ[k]
                if k == 0:
                    pe.wait_ge(hT_split, NP * g + NP)
                if isinstance(g, int) and g == 0 and k < NRING:
                    pe.wait_ge(setup_split, NSETUP)
                else:
                    pe.wait_ge(proj_split, NPROJ * g + k - NRING + 1)
                bank = ring[k % NRING]
                if kind == "u":
                    s = slice(j * R, (j + 1) * R)
                    terms = [(a[:, i, s], b[:, i, :]) for i in range(DC)
                             for a, b in parts(hT_hi[par], hT_lo[par], M_hi, M_lo)]
                else:
                    terms = [(a[:, ROW_AT[i] + j - i, :], b[:, i, :]) for i in range(j + 1)
                             for a, b in parts(T_hi[kind], T_lo[kind], hT_hi[par], hT_lo[par])]
                for n, (a, b) in enumerate(terms):
                    last = pe.matmul(bank[:, :], a, b, start=n == 0, stop=n == len(terms) - 1)
                last.then_inc(proj_done, 1)

            def gram(g, par, q):
                pe.wait_ge(proj_split, NPROJ * g + 2 * DC)
                if not (isinstance(g, int) and g == 0 and q == 0):
                    pe.wait_ge(p_copied, 2 * g + q)
                for pp in range(2):
                    s = slice((2 * q + pp) * R, (2 * q + pp + 1) * R)
                    terms = [(a[:, i, s], b[:, i, :, s]) for i in range(DC)
                             for a, b in parts(hT_hi[par], hT_lo[par], yT_hi, yT_lo)]
                    for n, (a, b) in enumerate(terms):
                        last = pe.matmul(p_ps[:, pp, :, :], a, b, start=n == 0, stop=n == len(terms) - 1)
                last.then_inc(gram_done, 1)

            def transpose_p(g, q):
                d = 2 * g + q
                pe.wait_ge(p_copied, d + 1)
                if q:
                    pe.wait_ge(s2_done, d)
                elif not (isinstance(g, int) and g == 0):
                    pe.wait_ge(kt_split, d)
                for pp in range(2):
                    for s in (L, G):
                        last = pe.transpose(pt_ps[:, pp, s, :], P_sb[q][:, pp, s, :], ident[:, :])
                last.then_inc(pt_done, 1)
                pe.wait_ge(cols_ready, d + 1)
                if not (isinstance(g, int) and g == 0 and q == 0):
                    pe.wait_ge(x0_done, d)
                for s, col in ((L, norms[q][:, 1, :]), (G, sq[q][:, G, :])):
                    for pp in range(2):
                        last = pe.transpose(row_ps[:, s, pp, :], col[:, pp:pp + 1].to_broadcast([R, R]), ident[:, :])
                last.then_inc(rows_done, 1)

            def transpose_k(g, q):
                pe.wait_ge(k_done, 2 * g + q + 1)
                pe.wait_ge(s2_done, 2 * g + 2)
                if q:
                    pe.wait_ge(kt_split, 2 * g + 1)
                for pp in range(2):
                    last = pe.transpose(kt_ps[:, pp, :], K_sb[:, pp, :], ident[:, :])
                last.then_inc(kt_done, 1)

            def apply_k(g, p):
                pe.wait_ge(kt_split, 2 * g + p // 2 + 1)
                pe.wait_ge(proj_split, NPROJ * g + 2 * DC + p + 1)
                if p:
                    pe.wait_ge(z_added, NP * g + p)
                for n, (a, b) in enumerate(parts(KT_hi, KT_lo, u_hi, u_lo)):
                    last = pe.matmul(bank_k[:, :], a[:, p % 2, :], b[:, p, :], start=n == 0, stop=n == 2)
                last.then_inc(ku_done, 1)

            def step(g, par, tail=True, ahead=True):
                project(g, par, 0)
                if tail:
                    transpose_p(g - 1, 0)
                project(g, par, 1)
                project(g, par, 2)
                project(g, par, 3)
                if tail:
                    transpose_p(g - 1, 1)
                project(g, par, 4)
                if tail:
                    transpose_k(g - 1, 0)
                project(g, par, 5)
                project(g, par, 6)
                if tail:
                    apply_k(g - 1, 0)
                    apply_k(g - 1, 1)
                if ahead:
                    layer0(g + 1, 0)
                project(g, par, 7)
                if tail:
                    transpose_k(g - 1, 1)
                if ahead:
                    layer0(g + 1, 1)
                project(g, par, 8)
                if tail:
                    apply_k(g - 1, 2)
                    apply_k(g - 1, 3)
                if ahead:
                    layer0(g + 1, 2)
                project(g, par, 9)
                if ahead:
                    layer0(g + 1, 3)
                gram(g, par, 0)
                project(g, par, 10)
                if ahead:
                    transpose_h(g + 1, 1 - par, 0)
                    if tail:
                        pe.wait_ge(z_added, NP * g)
                    transpose_h(g + 1, 1 - par, 1)
                project(g, par, 11)
                if ahead:
                    transpose_h(g + 1, 1 - par, 2)
                    transpose_h(g + 1, 1 - par, 3)
                gram(g, par, 1)

            pe.wait_ge(mix_steps, 6)
            for p in range(NP):
                layer0(0, p)
            at = 0

            def setup(shape_cols, terms):
                nonlocal at
                if at >= NRING:
                    pe.wait_ge(setup_split, at - NRING + 1)
                for n, (a, b) in enumerate(terms):
                    last = pe.matmul(ring[at % NRING][:, 0:shape_cols], a, b, start=n == 0, stop=n == len(terms) - 1)
                last.then_inc(setup_done, 1)
                at += 1

            for s in (L, G):
                pe.wait_ge(w_lo_done, s + 1)
                for i in range(DC):
                    setup(D - i * R, [(a[:, e, i * R:(i + 1) * R], b[:, e, i * R:D]) for e in range(DC)
                                      for a, b in parts(W_hi[s], W_lo[s], W_hi[s], W_lo[s])])
            for p in range(NP):
                transpose_h(0, 0, p)
            pe.wait_ge(w_loaded[3], 16)
            for e in range(DC):
                pe.wait_ge(setup_split, at - NRING + 1)
                for f in range(DC):
                    last = pe.transpose(ring[at % NRING][:, f * R:(f + 1) * R],
                                        w_raw[0][:, f, e * R:(e + 1) * R], ident[:, :])
                last.then_inc(setup_done, 1)
                at += 1
            pe.wait_ge(w_lo_done, 3)
            pe.wait_ge(setup_split, at)
            for i in range(DC):
                setup(D, [(a[:, e, i * R:(i + 1) * R], b[:, e, :]) for e in range(DC)
                          for a, b in parts(W_hi[2], W_lo[2], W_hi[3], W_lo[3])])

            step(0, 0, tail=False)
            step(1, 1)
            with pe.Fori(2, NG - 2, 2) as g:
                step(g, 0)
                step(g + 1, 1)
            step(NG - 2, 0)
            step(NG - 1, 1, ahead=False)
            transpose_p(NG - 1, 0)
            transpose_p(NG - 1, 1)
            transpose_k(NG - 1, 0)
            apply_k(NG - 1, 0)
            apply_k(NG - 1, 1)
            transpose_k(NG - 1, 1)
            apply_k(NG - 1, 2)
            apply_k(NG - 1, 3)

        def proj_dst(k, which):
            kind, j = PROJ[k]
            if kind == "u":
                return (u_hi, u_lo)[which][:, j, :]
            return (yT_hi, yT_lo)[which][:, j, kind, :]

        @block.scalar
        def _(act):
            def copy(dst, src, scale=1.0):
                return act.activation(dst, src, ACT.Copy, scale=scale)

            def split_x(g, c):
                if c == 0:
                    act.wait_ge(x_loaded, 16 * (g + 1))
                    if not (isinstance(g, int) and g == 0):
                        act.wait_ge(l0_done, NP * g)
                s = slice(2 * c, 2 * c + 2)
                copy(x_hi[:, s, :], x_sb[:, s, :]).then_inc(x_hi_done, 1)

            def normalise_h(g, par, p):
                act.wait_ge(y_scale, NP * g + p + 1)
                act.activation(h_sb[par][:, p, :], y_sb[:, p % 2, :], ACT.Identity, scale=y_rs[:, p:p + 1],
                               bias=y_nb[:, p:p + 1]).then_inc(h_ready, 1)

            def hi_hT(g, par, p):
                act.wait_ge(hT_done, NP * g + p + 1)
                bank = (bank_x, bank_k)[p % 2]
                copy(hT_hi[par][:, :, p * R:(p + 1) * R],
                     bank[:, :].rearrange("p (c r) -> p c r", c=DC)).then_inc(hT_hi_done, 1)

            def hi_proj(g, k):
                act.wait_ge(proj_done, NPROJ * g + k + 1)
                copy(proj_dst(k, 0), ring[k % NRING][:, :]).then_inc(proj_hi, 1)

            def copy_p(g, q):
                act.wait_ge(gram_done, 2 * g + q + 1)
                if not (isinstance(g, int) and g == 0):
                    act.wait_ge(s2_done, 2 * g + q - 1)
                copy(P_sb[q][:, :, :, :], p_ps).then_inc(p_copied, 1)

            def exp_g(g, q):
                act.wait_ge(negd_done, 2 * g + q + 1)
                for pp in range(2):
                    last = act.activation(E_g[:, pp, :], negd[:, pp, :], ACT.Exp, scale=neg_inv[:, 0:1],
                                          bias=exp_bias[q][:, pp:pp + 1])
                last.then_inc(exp_done, 1)

            def hi_kt(g, q):
                act.wait_ge(kt_done, 2 * g + q + 1)
                copy(KT_hi[:, :, :], kt_ps).then_inc(kt_hi_done, 1)

            def normalise_out(g, p):
                act.wait_ge(z_scale, NP * g + p + 1)
                if not (isinstance(g, int) and g == 0):
                    act.wait_ge(stored[p], 16 * g)
                act.activation(o_sb[:, p, :], z_sb[:, p % 2, :], ACT.Identity, scale=z_rs[:, p:p + 1],
                               bias=z_nb[:, p:p + 1]).then_inc(o_ready, 1)

            def step(g, par, tail=True, ahead=True, ahead2=True):
                hi_proj(g, 0)
                hi_proj(g, 1)
                if tail:
                    exp_g(g - 1, 0)
                hi_proj(g, 2)
                hi_proj(g, 3)
                hi_proj(g, 4)
                if tail:
                    exp_g(g - 1, 1)
                    hi_kt(g - 1, 0)
                hi_proj(g, 5)
                hi_proj(g, 6)
                if tail:
                    normalise_out(g - 1, 0)
                hi_proj(g, 7)
                if tail:
                    normalise_out(g - 1, 1)
                    hi_kt(g - 1, 1)
                if ahead:
                    normalise_h(g + 1, 1 - par, 0)
                hi_proj(g, 8)
                if ahead:
                    normalise_h(g + 1, 1 - par, 1)
                if tail:
                    normalise_out(g - 1, 2)
                    normalise_out(g - 1, 3)
                if ahead:
                    normalise_h(g + 1, 1 - par, 2)
                hi_proj(g, 9)
                if ahead:
                    normalise_h(g + 1, 1 - par, 3)
                copy_p(g, 0)
                if ahead2:
                    split_x(g + 2, 0)
                hi_proj(g, 10)
                if ahead:
                    hi_hT(g + 1, 1 - par, 0)
                    hi_hT(g + 1, 1 - par, 1)
                if ahead2:
                    split_x(g + 2, 1)
                hi_proj(g, 11)
                if ahead:
                    hi_hT(g + 1, 1 - par, 2)
                    hi_hT(g + 1, 1 - par, 3)
                copy_p(g, 1)

            act.wait_ge(mix_steps, 4)
            copy(mix_hi[:, :], mix[:, :]).then_inc(mix_steps, 1)
            split_x(0, 0)
            split_x(0, 1)
            act.wait_ge(gates_loaded, 32)
            act.activation(gate_e[:, 0:1], gates[:, 0:1], ACT.Exp, scale=-1.0)
            act.activation(gate_e[:, 1:2], gates[:, 1:2], ACT.Exp).then_inc(gate_exp, 1)
            for i in range(2):
                act.wait_ge(w_loaded[i], 16)
                copy(W_hi[i], w_raw[i][:, :, :]).then_inc(w_hi_done, 1)
            for p in range(NP):
                normalise_h(0, 0, p)
            act.wait_ge(w_loaded[2], 16)
            copy(W_hi[2], w_raw[2][:, :, :]).then_inc(w_hi_done, 1)
            at = 0
            for s in (L, G):
                for i in range(DC):
                    act.wait_ge(setup_done, at + 1)
                    bank = ring[at % NRING]
                    last = copy(T_hi[s][:, ROW_AT[i], :], bank[:, 0:R])
                    if i < DC - 1:
                        last = copy(T_hi[s][:, ROW_AT[i] + 1:ROW_AT[i] + DC - i, :],
                                    bank[:, R:D - i * R].rearrange("p (b c) -> p b c", c=R), scale=2.0)
                    last.then_inc(setup_hi, 1)
                    at += 1
            for p in range(NP):
                hi_hT(0, 0, p)
            for dst in (W_hi[3], M_hi[:, :, :]):
                for i in range(DC):
                    act.wait_ge(setup_done, at + 1)
                    copy(dst[:, i, :], ring[at % NRING][:, :]).then_inc(setup_hi, 1)
                    at += 1
            split_x(1, 0)
            split_x(1, 1)

            step(0, 0, tail=False)
            step(1, 1)
            with act.Fori(2, NG - 2, 2) as g:
                step(g, 0)
                step(g + 1, 1)
            step(NG - 2, 0, ahead2=False)
            step(NG - 1, 1, ahead=False, ahead2=False)
            exp_g(NG - 1, 0)
            exp_g(NG - 1, 1)
            hi_kt(NG - 1, 0)
            normalise_out(NG - 1, 0)
            hi_kt(NG - 1, 1)
            normalise_out(NG - 1, 1)
            normalise_out(NG - 1, 2)
            normalise_out(NG - 1, 3)

        @block.vector
        def _(dve):
            def add_y(g, p):
                dve.wait_ge(l0_done, NP * g + p + 1)
                if not (isinstance(g, int) and g == 0 and p < 2):
                    dve.wait_ge(h_ready, NP * g + p - 1)
                dve.tensor_tensor(y_sb[:, p % 2, :], bank_x[:, :], bias_bc[:, :], ALU.add).then_inc(y_added, 1)
                dve.wait_ge(y_added, NP * g + p + 1)
                dve.bn_stats(y_bn[:, p, :], y_sb[:, p % 2, :]).then_inc(y_counted, 1)
                dve.wait_ge(y_counted, NP * g + p + 1)
                settle(dve)
                dve.bn_aggr(y_mv[:, p, :], y_bn[:, p, :]).then_inc(y_stats, 1)

            def lo_hT(g, par, p):
                dve.wait_ge(hT_hi_done, NP * g + p + 1)
                bank = (bank_x, bank_k)[p % 2]
                s = slice(p * R, (p + 1) * R)
                dve.tensor_tensor(hT_lo[par][:, :, s], bank[:, :].rearrange("p (c r) -> p c r", c=DC),
                                  hT_hi[par][:, :, s], ALU.subtract).then_inc(hT_split, 1)

            def lo_proj(g, k):
                dve.wait_ge(proj_hi, NPROJ * g + k + 1)
                dve.tensor_tensor(proj_dst(k, 1), ring[k % NRING][:, :], proj_dst(k, 0),
                                  ALU.subtract).then_inc(proj_split, 1)

            def diagonals(g, q):
                dve.wait_ge(p_copied, 2 * g + q + 1)
                if q:
                    dve.wait_ge(sq_done, 2 * g + q)
                for pp in range(2):
                    for s in (L, G):
                        last = dve.tensor_tensor_reduce(
                            out=diag_scr[:, 2 * pp + s, :], in0=P_sb[q][:, pp, s, :], in1=ident[:, :], scale=1.0,
                            scalar=0.0, op0=ALU.mult, op1=ALU.add, accum_out=sq[q][:, s, pp:pp + 1])
                last.then_inc(sq_done, 1)

            def similarities(g, q):
                d = 2 * g + q
                dve.wait_ge(pt_done, d + 1)
                dve.tensor_tensor(S2[:, :, :, :], pt_ps, P_sb[q][:, :, :, :], ALU.add).then_inc(s2_done, 1)
                dve.wait_ge(rows_done, d + 1)
                dve.wait_ge(s2_done, d + 1)
                dve.scalar_tensor_tensor(negd[:, :, :], S2[:, :, G, :], -1.0, row_ps[:, G, :, :], ALU.mult,
                                         ALU.add).then_inc(negd_done, 1)
                dve.scalar_tensor_tensor(X0[:, :, :], S2[:, :, L, :], 0.0, row_ps[:, L, :, :], ALU.max,
                                         ALU.mult).then_inc(x0_done, 1)
                dve.wait_ge(x0_done, d + 1)
                for pp in range(2):
                    last = dve.tensor_tensor_reduce(
                        out=X_l[:, pp, :], in0=X0[:, pp, :], in1=mask[:, :], scale=1.0, scalar=0.0,
                        op0=ALU.mult, op1=ALU.add, accum_out=sums[:, pp:pp + 1])
                last.then_inc(xl_done, 1)

            def coefficients(g, q):
                d = 2 * g + q
                dve.wait_ge(exp_done, d + 1)
                for pp in range(2):
                    last = dve.scalar_tensor_tensor(X_g[:, pp, :], E_g[:, pp, :], 1.0, mask[:, :], ALU.min, ALU.mult,
                                                    accum_out=sums[:, 2 + pp:3 + pp])
                last.then_inc(xg_done, 1)
                dve.wait_ge(xg_done, d + 1)
                dve.wait_ge(xl_done, d + 1)
                dve.tensor_tensor(dens[:, :], sums[:, :], floors[q][:, :], ALU.max).then_inc(dens_done, 1)
                dve.wait_ge(dens_done, d + 1)
                dve.reciprocal(recs[:, :], dens[:, :]).then_inc(recs_done, 1)
                dve.wait_ge(recs_done, d + 1)
                dve.tensor_tensor(coef[:, :], recs[:, :], mixw[:, :], ALU.mult).then_inc(coef_done, 1)

            def combine(g, q):
                dve.wait_ge(coef_done, 2 * g + q + 1)
                dve.wait_ge(kl_done, 2 * g + q + 1)
                for pp in range(2):
                    last = dve.scalar_tensor_tensor(K_sb[:, pp, :], X_g[:, pp, :], coef[:, 2 + pp:3 + pp],
                                                    K_l[:, pp, :], ALU.mult, ALU.add)
                last.then_inc(k_done, 1)

            def lo_kt(g, q):
                dve.wait_ge(kt_hi_done, 2 * g + q + 1)
                dve.tensor_tensor(KT_lo[:, :, :], kt_ps, KT_hi[:, :, :], ALU.subtract).then_inc(kt_split, 1)

            def add_z(g, par, p):
                t = NP * g + p
                dve.wait_ge(ku_done, t + 1)
                if not (isinstance(g, int) and g == 0 and p < 2):
                    dve.wait_ge(o_ready, t - 1)
                dve.tensor_tensor(z_sb[:, p % 2, :], bank_k[:, :], h_sb[par][:, p, :], ALU.add).then_inc(z_added, 1)
                dve.wait_ge(z_added, t + 1)
                dve.bn_stats(z_bn[:, p, :], z_sb[:, p % 2, :]).then_inc(z_counted, 1)
                dve.wait_ge(z_counted, t + 1)
                settle(dve)
                dve.bn_aggr(z_mv[:, p, :], z_bn[:, p, :]).then_inc(z_stats, 1)

            def step(g, par, tail=True, ahead=True):
                if tail:
                    diagonals(g - 1, 1)
                lo_proj(g, 0)
                if tail:
                    similarities(g - 1, 0)
                lo_proj(g, 1)
                lo_proj(g, 2)
                if tail:
                    coefficients(g - 1, 0)
                lo_proj(g, 3)
                if tail:
                    combine(g - 1, 0)
                    similarities(g - 1, 1)
                lo_proj(g, 4)
                if tail:
                    coefficients(g - 1, 1)
                    lo_kt(g - 1, 0)
                lo_proj(g, 5)
                if tail:
                    combine(g - 1, 1)
                lo_proj(g, 6)
                if tail:
                    add_z(g - 1, 1 - par, 0)
                    add_z(g - 1, 1 - par, 1)
                if ahead:
                    add_y(g + 1, 0)
                lo_proj(g, 7)
                if tail:
                    lo_kt(g - 1, 1)
                if ahead:
                    add_y(g + 1, 1)
                lo_proj(g, 8)
                if tail:
                    add_z(g - 1, 1 - par, 2)
                    add_z(g - 1, 1 - par, 3)
                if ahead:
                    add_y(g + 1, 2)
                lo_proj(g, 9)
                if ahead:
                    add_y(g + 1, 3)
                diagonals(g, 0)
                lo_proj(g, 10)
                if ahead:
                    lo_hT(g + 1, 1 - par, 0)
                    lo_hT(g + 1, 1 - par, 1)
                lo_proj(g, 11)
                if ahead:
                    lo_hT(g + 1, 1 - par, 2)
                    lo_hT(g + 1, 1 - par, 3)

            dve.wait_ge(ident_ready, 2)
            dve.tensor_scalar(off_diag[:, :], ident[:, :], -1.0, 1.0, ALU.mult, ALU.add).then_inc(mix_steps, 1)
            dve.wait_ge(adj_loaded, 32)
            dve.tensor_tensor(mix[:, :], adj_bd[:, :], adj_bd[:, :], ALU.mult).then_inc(mix_steps, 1)
            dve.wait_ge(mix_steps, 2)
            dve.tensor_tensor(mix[:, :], mix[:, :], ident[:, :], ALU.add).then_inc(mix_steps, 1)
            dve.tensor_tensor(mask[:, :], adj_bd[:, :], off_diag[:, :], ALU.mult).then_inc(mix_steps, 1)
            dve.wait_ge(mix_steps, 5)
            dve.tensor_tensor(mix_lo[:, :], mix[:, :], mix_hi[:, :], ALU.subtract).then_inc(mix_steps, 1)
            dve.wait_ge(gate_exp, 1)
            dve.tensor_scalar(gate_t[:, 0:1], gate_e[:, 0:1], 1.0, None, ALU.add)
            dve.scalar_tensor_tensor(gate_t[:, 1:2], gate_e[:, 1:2], -2.0, gate_e[:, 1:2], ALU.mult,
                                     ALU.mult).then_inc(gate_steps, 1)
            dve.wait_ge(gate_steps, 1)
            dve.reciprocal(gate_t[:, 2:4], gate_t[:, 0:2]).then_inc(gate_steps, 1)
            dve.wait_ge(gate_steps, 2)
            dve.tensor_copy(neg_inv[:, :], gate_t[:, 3:4])
            dve.tensor_copy(mixw[:, 0:2], gate_t[:, 2:3].to_broadcast([R, 2]))
            dve.tensor_scalar(mixw[:, 2:4], gate_t[:, 2:3].to_broadcast([R, 2]), -1.0, 1.0, ALU.mult,
                              ALU.add).then_inc(gate_steps, 1)
            dve.wait_ge(gate_steps, 3)
            dve.wait_ge(bias_loaded, 16)
            for p in range(2):
                add_y(0, p)
            for i in range(2):
                dve.wait_ge(w_hi_done, i + 1)
                dve.tensor_tensor(W_lo[i], w_raw[i][:, :, :], W_hi[i], ALU.subtract).then_inc(w_lo_done, 1)
            for p in range(2, NP):
                add_y(0, p)
            dve.wait_ge(w_hi_done, 3)
            dve.tensor_tensor(W_lo[2], w_raw[2][:, :, :], W_hi[2], ALU.subtract).then_inc(w_lo_done, 1)
            at = 0
            for s in (L, G):
                for i in range(DC):
                    dve.wait_ge(setup_hi, at + 1)
                    bank = ring[at % NRING]
                    first = ROW_AT[i]
                    last = dve.tensor_tensor(T_lo[s][:, first, :], bank[:, 0:R], T_hi[s][:, first, :], ALU.subtract)
                    if i < DC - 1:
                        b = slice(first + 1, first + DC - i)
                        last = dve.scalar_tensor_tensor(
                            T_lo[s][:, b, :], bank[:, R:D - i * R].rearrange("p (b c) -> p b c", c=R), 2.0,
                            T_hi[s][:, b, :], ALU.mult, ALU.subtract)
                    last.then_inc(setup_split, 1)
                    at += 1
            for p in range(NP):
                lo_hT(0, 0, p)
            for hi, lo in ((W_hi[3], W_lo[3]), (M_hi[:, :, :], M_lo[:, :, :])):
                for i in range(DC):
                    dve.wait_ge(setup_hi, at + 1)
                    dve.tensor_tensor(lo[:, i, :], ring[at % NRING][:, :], hi[:, i, :],
                                      ALU.subtract).then_inc(setup_split, 1)
                    at += 1

            step(0, 0, tail=False)
            step(1, 1)
            with dve.Fori(2, NG - 2, 2) as g:
                step(g, 0)
                step(g + 1, 1)
            step(NG - 2, 0)
            step(NG - 1, 1, ahead=False)
            diagonals(NG - 1, 1)
            similarities(NG - 1, 0)
            coefficients(NG - 1, 0)
            combine(NG - 1, 0)
            similarities(NG - 1, 1)
            coefficients(NG - 1, 1)
            lo_kt(NG - 1, 0)
            combine(NG - 1, 1)
            add_z(NG - 1, 1, 0)
            add_z(NG - 1, 1, 1)
            lo_kt(NG - 1, 1)
            add_z(NG - 1, 1, 2)
            add_z(NG - 1, 1, 3)

        @block.gpsimd
        def _(pool):
            def split_x(g, p):
                pool.wait_ge(x_hi_done, 2 * g + p // 2 + 1)
                pool.tensor_tensor(x_lo[:, p, :], x_sb[:, p, :], x_hi[:, p, :], ALU.subtract).then_inc(x_lo_done, 1)

            def scale_of(stats, ve_done, rs_done, scale, mv, ve, rs, nb, t, p):
                pool.wait_ge(stats, t + 1)
                settle(pool)
                pool.tensor_scalar(ve[:, p:p + 1], mv[:, p, 1:2], LN_EPS, None, ALU.add).then_inc(ve_done, 1)
                pool.wait_ge(ve_done, t + 1)
                pool.tensor_tensor(rs[:, p:p + 1], ve[:, p:p + 1], pow_half[:, 2:3], ALU.pow).then_inc(rs_done, 1)
                pool.wait_ge(rs_done, t + 1)
                settle(pool)
                pool.tensor_scalar(nb[:, p:p + 1], mv[:, p, 0:1], rs[:, p:p + 1], -1.0, ALU.mult,
                                   ALU.mult).then_inc(scale, 1)

            def scale_y(g, p):
                scale_of(y_stats, y_ve_done, y_rs_done, y_scale, y_mv, y_ve, y_rs, y_nb, NP * g + p, p)

            def scale_z(g, p):
                scale_of(z_stats, z_ve_done, z_rs_done, z_scale, z_mv, z_ve, z_rs, z_nb, NP * g + p, p)

            def columns(g, q):
                d = 2 * g + q
                pool.wait_ge(sq_done, d + 1)
                settle(pool)
                for c in range(2):
                    last = pool.tensor_scalar(sq_floor[q][:, c, :], sq[q][:, L, :], EPS * EPS, None, ALU.max)
                last.then_inc(floor_done, 1)
                pool.tensor_scalar(exp_bias[q][:, :], sq[q][:, G, :], neg_inv[:, 0:1], None, ALU.mult)
                pool.wait_ge(floor_done, d + 1)
                pool.tensor_tensor(norms[q][:, :, :], sq_floor[q][:, :, :],
                                   pow_half[:, :].rearrange("r (a b) -> r a b", a=2), ALU.pow).then_inc(norm_done, 1)
                pool.wait_ge(norm_done, d + 1)
                settle(pool)
                pool.tensor_scalar(floors[q][:, 0:2], norms[q][:, 0, :], 2 * EPS, None, ALU.mult).then_inc(cols_ready, 1)

            def scale_l(g, q):
                pool.wait_ge(coef_done, 2 * g + q + 1)
                settle(pool)
                for pp in range(2):
                    last = pool.tensor_scalar(K_l[:, pp, :], X_l[:, pp, :], coef[:, pp:pp + 1], None, ALU.mult)
                last.then_inc(kl_done, 1)

            def step(g, tail=True, ahead=True, ahead2=True):
                if tail:
                    columns(g - 1, 1)
                    scale_l(g - 1, 0)
                    scale_l(g - 1, 1)
                    scale_z(g - 1, 0)
                    scale_z(g - 1, 1)
                if ahead:
                    scale_y(g + 1, 0)
                    scale_y(g + 1, 1)
                if tail:
                    scale_z(g - 1, 2)
                    scale_z(g - 1, 3)
                if ahead:
                    scale_y(g + 1, 2)
                    scale_y(g + 1, 3)
                columns(g, 0)
                if ahead2:
                    for p in range(NP):
                        split_x(g + 2, p)

            pool.memset(adj_bd[:, :], 0.0).then_inc(adj_zeroed, 1)
            pool.memset(ident[:, :], 0.0).then_inc(ident_ready, 1)
            pool.wait_ge(ident_ready, 1)
            pool.affine_select(out=ident[:, :], in_=ident[:, :], compare_op=ALU.not_equal, fill=1.0, base=0,
                               pattern=[[-1, R]], channel_multiplier=1).then_inc(ident_ready, 1)
            pool.memset(pow_half[:, 0:2], 0.5)
            pool.memset(pow_half[:, 2:4], -0.5)
            pool.memset(floors[0][:, 2:4], EPS)
            pool.memset(floors[1][:, 2:4], EPS).then_inc(pow_ready, 1)
            pool.wait_ge(pow_ready, 1)
            for p in range(NP):
                split_x(0, p)
            for p in range(NP):
                scale_y(0, p)
            pool.wait_ge(gate_steps, 3)
            for p in range(NP):
                split_x(1, p)

            step(0, tail=False)
            step(1)
            with pool.Fori(2, NG - 2, 1) as g:
                step(g)
            step(NG - 2, ahead2=False)
            step(NG - 1, ahead=False, ahead2=False)
            columns(NG - 1, 1)
            scale_l(NG - 1, 0)
            scale_l(NG - 1, 1)
            for p in range(NP):
                scale_z(NG - 1, p)


_INS = ['x', 'adj', 'L0_gnn_bias', 'L1_gnn_W_lang', 'L1_gnn_W_grav', 'L1_gnn_W_V', 'L1_gnn_W_O', 'L1_gnn_gate_logit',
        'L1_gnn_log_sigma']
_OUTS = [((128, 64, 512), 'float32')]


def kernel(**inputs):
    import numpy as _np
    import concourse.bacc as _bacc
    from concourse import mybir as _mybir
    from concourse.bass_utils import run_bass_kernel_spmd as _run

    nc = _bacc.Bacc("TRN2", target_bir_lowering=False, num_devices=1)
    arrays, args = {}, []
    for name in _INS:
        a = _np.ascontiguousarray(inputs[name])
        arrays[f"in_{name}_dram"] = a
        args.append(nc.dram_tensor(f"in_{name}_dram", a.shape, _mybir.dt.from_np(a.dtype), kind="ExternalInput").ap())
    for i, (shape, dtype) in enumerate(_OUTS):
        dt = _mybir.dt.from_np(_np.dtype(dtype))
        args.append(nc.dram_tensor(f"out_{i}_dram", shape, dt, kind="ExternalOutput").ap())
    bass_two_layer_graph_resnorm(nc, *args)
    r = _run(nc, [arrays], core_ids=[0])
    got = tuple(r.results[0][f"out_{i}_dram"] for i in range(len(_OUTS)))
    return got[0]
```

```python
import concourse.bass as bass
from concourse import mybir
from contextlib import ExitStack


def bass_two_layer_graph_resnorm(
    nc: bass.Bass,
    x: bass.AP,
    adj: bass.AP,
    bias: bass.AP,
    w_lang: bass.AP,
    w_grav: bass.AP,
    w_v: bass.AP,
    w_o: bass.AP,
    gate_logit: bass.AP,
    log_sigma: bass.AP,
    out: bass.AP,
):
    fp32 = mybir.dt.float32
    fp32r = mybir.dt.float32r
    ALU = mybir.AluOpType
    ACT = mybir.ActivationFunctionType

    B, N, D = x.shape
    R = 128
    NP = 4
    NG = B * N // (R * NP)
    DC = D // R
    GT = NP * R
    LN_EPS = 1e-5
    EPS = 1e-8
    L, G = 0, 1
    NBLK = DC * (DC + 1) // 2
    ROW_AT = [i * DC - i * (i - 1) // 2 for i in range(DC)]
    PROJ = [(L, 3), (L, 0), (L, 2), (L, 1), (G, 3), (G, 0), (G, 2), (G, 1)] + [("u", p) for p in range(NP)]
    NPROJ = len(PROJ)
    NRING = 3
    NSETUP = 2 * DC + 2 * DC
    assert NG % 2 == 0 and NPROJ % NRING == 0

    def ring_of(k):
        return (NSETUP + k) % NRING

    x_v = x.rearrange("(g p b) n f -> g (b n) p f", p=NP, b=2)
    out_v = out.rearrange("(g p b) n f -> g (b n) p f", p=NP, b=2)

    ctx = ExitStack()
    with ctx:
        def sb(name, shape, dt=fp32):
            return ctx.enter_context(nc.sbuf_tensor(name, shape, dt))

        def pb(name):
            return ctx.enter_context(nc.psum_tensor(name, [R, 512], fp32))

        def sem(name):
            return ctx.enter_context(nc.semaphore(name))

        ident = sb("ident", [R, R])
        off_diag = sb("off_diag", [R, R])
        adj_bd = sb("adj_bd", [R, R])
        mask = sb("mask", [R, R])
        mix = sb("mix", [R, R])
        mix_hi = sb("mix_hi", [R, R], fp32r)
        mix_lo = sb("mix_lo", [R, R], fp32r)
        bias_bc = sb("bias_bc", [R, D])
        gates = sb("gates", [R, 2])
        gate_e = sb("gate_e", [R, 2])
        gate_t = sb("gate_t", [R, 4])
        neg_inv = sb("neg_inv", [R, 1])
        mixw = sb("mixw", [R, 4])
        pow_half = sb("pow_half", [R, 4])
        T_hi = [sb(f"T_hi{s}", [R, NBLK, R], fp32r) for s in (L, G)]
        T_lo = [sb(f"T_lo{s}", [R, NBLK, R], fp32r) for s in (L, G)]
        M_hi = sb("M_hi", [R, DC, D], fp32r)
        M_lo = sb("M_lo", [R, DC, D], fp32r)
        x_sb = sb("x_sb", [R, NP, D])
        x_hi = sb("x_hi", [R, NP, D], fp32r)
        x_lo = sb("x_lo", [R, NP, D], fp32r)
        h_sb = [sb(f"h_sb{i}", [R, NP, D]) for i in range(2)]
        hT_hi = [sb(f"hT_hi{i}", [R, DC, GT], fp32r) for i in range(2)]
        hT_lo = [sb(f"hT_lo{i}", [R, DC, GT], fp32r) for i in range(2)]
        yT_hi = sb("yT_hi", [R, DC, 2, GT], fp32r)
        yT_lo = sb("yT_lo", [R, DC, 2, GT], fp32r)
        u_hi = sb("u_hi", [R, NP, D], fp32r)
        u_lo = sb("u_lo", [R, NP, D], fp32r)
        P_sb = [sb(f"P_sb{q}", [R, 2, 2, R]) for q in range(2)]
        diag_scr = sb("diag_scr", [R, 4, R])
        S2 = sb("S2", [R, 2, 2, R])
        X0 = sb("X0", [R, 2, R])
        X_l = sb("X_l", [R, 2, R])
        negd = sb("negd", [R, 2, R])
        E_g = sb("E_g", [R, 2, R])
        X_g = sb("X_g", [R, 2, R])
        K_l = sb("K_l", [R, 2, R])
        K_sb = sb("K_sb", [R, 2, R])
        KT_hi = sb("KT_hi", [R, 2, R], fp32r)
        KT_lo = sb("KT_lo", [R, 2, R], fp32r)
        sq = [sb(f"sq{q}", [R, 2, 2]) for q in range(2)]
        sq_floor = [sb(f"sq_floor{q}", [R, 2, 2]) for q in range(2)]
        norms = [sb(f"norms{q}", [R, 2, 2]) for q in range(2)]
        exp_bias = [sb(f"exp_bias{q}", [R, 2]) for q in range(2)]
        floors = [sb(f"floors{q}", [R, 4]) for q in range(2)]
        sums = sb("sums", [R, 4])
        dens = sb("dens", [R, 4])
        recs = sb("recs", [R, 4])
        coef = sb("coef", [R, 4])
        y_bn = sb("y_bn", [R, NP, 6])
        y_mv = sb("y_mv", [R, NP, 2])
        y_ve = sb("y_ve", [R, NP])
        y_nm = sb("y_nm", [R, NP])
        y_rs = sb("y_rs", [R, NP])
        y_nb = sb("y_nb", [R, NP])
        z_bn = sb("z_bn", [R, NP, 6])
        z_mv = sb("z_mv", [R, NP, 2])
        z_ve = sb("z_ve", [R, NP])
        z_nm = sb("z_nm", [R, NP])
        z_rs = sb("z_rs", [R, NP])
        z_nb = sb("z_nb", [R, NP])
        o_sb = sb("o_sb", [R, NP, D])
        w_raw = [sb("w_raw", [R, DC, D]), o_sb, h_sb[1]]
        yT_w = [t[:, :, :, :].rearrange("p a s t -> p (a s t)") for t in (yT_hi, yT_lo)]

        def half(view, k):
            return view[:, k * DC * D:(k + 1) * DC * D].rearrange("p (c d) -> p c d", c=DC)

        W_hi = [half(yT_w[0], 0), half(yT_w[0], 1), u_hi[:, :, :], hT_hi[1][:, :, :]]
        W_lo = [half(yT_w[1], 0), half(yT_w[1], 1), u_lo[:, :, :], hT_lo[1][:, :, :]]

        ring = [pb(f"ring{i}") for i in range(NRING)]
        bank_x = pb("bank_x")
        bank_k = pb("bank_k")
        bank_p = pb("bank_p")
        bank_pt = pb("bank_pt")
        bank_r = pb("bank_r")
        hT_banks = [bank_x, bank_k, bank_pt, bank_r]
        p_ps = bank_p[:, :].rearrange("r (p s c) -> r p s c", p=2, s=2)
        pt_ps = bank_pt[:, :].rearrange("r (p s c) -> r p s c", p=2, s=2)
        row_ps = bank_r[:, :].rearrange("r (s p c) -> r s p c", p=2, s=2)
        kt_ps = bank_pt[:, 0:2 * R].rearrange("r (p c) -> r p c", p=2)

        w_loaded = [sem(f"w_loaded{i}") for i in range(4)]
        adj_zeroed = sem("adj_zeroed")
        adj_loaded = sem("adj_loaded")
        bias_loaded = sem("bias_loaded")
        gates_loaded = sem("gates_loaded")
        ident_ready = sem("ident_ready")
        pow_ready = sem("pow_ready")
        mix_steps = sem("mix_steps")
        gate_exp = sem("gate_exp")
        gate_steps = sem("gate_steps")
        w_hi_done = sem("w_hi_done")
        w_lo_done = sem("w_lo_done")
        setup_done = sem("setup_done")
        setup_hi = sem("setup_hi")
        setup_split = sem("setup_split")
        x0_loaded = [sem(f"x0_loaded{c}") for c in range(2)]
        x_loaded = sem("x_loaded")
        x_hi_done = sem("x_hi_done")
        x_lo_done = sem("x_lo_done")
        l0_done = sem("l0_done")
        y_added = sem("y_added")
        y_counted = sem("y_counted")
        y_stats = sem("y_stats")
        y_ve_done = sem("y_ve_done")
        y_rs_done = sem("y_rs_done")
        y_scale = sem("y_scale")
        h_ready = sem("h_ready")
        hT_done = sem("hT_done")
        hT_hi_done = sem("hT_hi_done")
        hT_split = sem("hT_split")
        proj_done = sem("proj_done")
        proj_hi = sem("proj_hi")
        proj_split = sem("proj_split")
        gram_done = sem("gram_done")
        p_copied = sem("p_copied")
        sq_done = sem("sq_done")
        floor_done = sem("floor_done")
        norm_done = sem("norm_done")
        cols_ready = sem("cols_ready")
        pt_done = sem("pt_done")
        rows_done = sem("rows_done")
        s2_done = sem("s2_done")
        x0_done = sem("x0_done")
        xl_done = sem("xl_done")
        negd_done = sem("negd_done")
        exp_done = sem("exp_done")
        xg_done = sem("xg_done")
        dens_done = sem("dens_done")
        recs_done = sem("recs_done")
        coef_done = sem("coef_done")
        kl_done = sem("kl_done")
        k_done = sem("k_done")
        kt_done = sem("kt_done")
        kt_hi_done = sem("kt_hi_done")
        kt_split = sem("kt_split")
        ku_done = sem("ku_done")
        z_added = sem("z_added")
        z_counted = sem("z_counted")
        z_stats = sem("z_stats")
        z_ve_done = sem("z_ve_done")
        z_rs_done = sem("z_rs_done")
        z_scale = sem("z_scale")
        o_ready = sem("o_ready")
        stored = [sem(f"stored{p}") for p in range(NP)]

        block = ctx.enter_context(nc.Block())

        def parts(hi, lo, hi2, lo2):
            return [(hi, hi2), (hi, lo2), (lo, hi2)]

        def settle(engine):
            engine.nop(nofuse=True)

        @block.sync
        def _(sp):
            sp.wait_ge(adj_zeroed, 1)
            for b in range(2):
                s = slice(b * N, (b + 1) * N)
                sp.dma_start(adj_bd[s, s], adj).then_inc(adj_loaded, 16)
            for c in range(2):
                s = slice(2 * c, 2 * c + 2)
                sp.dma_start(x_sb[:, s, :], x_v[0][:, s, :]).then_inc(x0_loaded[c], 16)
            sp.dma_start(w_raw[0][:, :, :], w_lang.rearrange("(c p) d -> p c d", p=R)).then_inc(w_loaded[0], 16)
            sp.dma_start(gates[:, 0:1], gate_logit.partition_broadcast(R)).then_inc(gates_loaded, 16)
            sp.dma_start(gates[:, 1:2], log_sigma.partition_broadcast(R)).then_inc(gates_loaded, 16)
            sp.dma_start(bias_bc[:, :], bias.partition_broadcast(R)).then_inc(bias_loaded, 16)
            for i, w in ((1, w_grav), (2, w_v)):
                sp.dma_start(w_raw[i][:, :, :], w.rearrange("(c p) d -> p c d", p=R)).then_inc(w_loaded[i], 16)
            sp.wait_ge(w_lo_done, DC)
            sp.dma_start(w_raw[0][:, :, :], w_o.rearrange("(c p) d -> p c d", p=R)).then_inc(w_loaded[3], 16)
            sp.wait_ge(x_lo_done, NP)
            sp.dma_start(x_sb[:, :, :], x_v[1]).then_inc(x_loaded, 16)

            def load(g):
                sp.wait_ge(x_lo_done, NP * g)
                sp.dma_start(x_sb[:, :, :], x_v[g]).then_inc(x_loaded, 16)

            def store(g):
                for p in range(NP):
                    sp.wait_ge(o_ready, NP * g + p + 1)
                    sp.dma_start(out_v[g][:, p, :], o_sb[:, p, :]).then_inc(stored[p], 16)

            load(2)
            with sp.Fori(1, NG - 2, 1) as g:
                load(g + 2)
                store(g - 1)
            store(NG - 3)
            store(NG - 2)
            store(NG - 1)
            for p in range(NP):
                sp.wait_ge(stored[p], 16 * NG)

        @block.tensor
        def _(pe):
            def layer0(g, p):
                pe.wait_ge(x_lo_done, NP * g + p + 1)
                if p >= 2:
                    pe.wait_ge(y_added, NP * g + p - 1)
                elif p == 1 and not (isinstance(g, int) and g < 2):
                    pe.wait_ge(p_copied, 2 * g - 2)
                bank = (bank_x, bank_p)[p % 2]
                for n, (w, r) in enumerate(parts(mix_hi, mix_lo, x_hi, x_lo)):
                    last = pe.matmul(bank[:, :], w[:, :], r[:, p, :], start=n == 0, stop=n == 2)
                last.then_inc(l0_done, 1)

            def transpose_h(g, par, p):
                pe.wait_ge(h_ready, NP * g + p + 1)
                if p == 0:
                    pe.wait_ge(y_added, NP * g + 3)
                elif isinstance(g, int) and g < 2:
                    pass
                elif p == 2:
                    pe.wait_ge(kt_split, 2 * g - 2)
                else:
                    pe.wait_ge(z_added, NP * g - NP)
                for c in range(DC):
                    last = pe.transpose(hT_banks[p][:, c * R:(c + 1) * R], h_sb[par][:, p, c * R:(c + 1) * R], ident[:, :])
                last.then_inc(hT_done, 1)

            def project(g, par, k):
                kind, j = PROJ[k]
                if k == 0:
                    pe.wait_ge(hT_split, NP * g + NP)
                if isinstance(g, int) and g == 0 and k < NRING:
                    pe.wait_ge(setup_split, NSETUP - NRING + 1 + k)
                else:
                    pe.wait_ge(proj_split, NPROJ * g + k - NRING + 1)
                bank = ring[ring_of(k)]
                if kind == "u":
                    s = slice(j * R, (j + 1) * R)
                    terms = [(a[:, i, s], b[:, i, :]) for i in range(DC)
                             for a, b in parts(hT_hi[par], hT_lo[par], M_hi, M_lo)]
                else:
                    terms = [(a[:, ROW_AT[i] + j - i, :], b[:, i, :]) for i in range(j + 1)
                             for a, b in parts(T_hi[kind], T_lo[kind], hT_hi[par], hT_lo[par])]
                for n, (a, b) in enumerate(terms):
                    last = pe.matmul(bank[:, :], a, b, start=n == 0, stop=n == len(terms) - 1)
                last.then_inc(proj_done, 1)

            def gram(g, par, q):
                pe.wait_ge(proj_split, NPROJ * g + 2 * DC)
                if q:
                    pe.wait_ge(p_copied, 2 * g + q)
                elif isinstance(g, int) and g == NG - 1:
                    pe.wait_ge(p_copied, 2 * g)
                else:
                    pe.wait_ge(y_added, NP * g + 2 * NP)
                for pp in range(2):
                    s = slice((2 * q + pp) * R, (2 * q + pp + 1) * R)
                    terms = [(a[:, i, s], b[:, i, :, s]) for i in range(DC)
                             for a, b in parts(hT_hi[par], hT_lo[par], yT_hi, yT_lo)]
                    for n, (a, b) in enumerate(terms):
                        last = pe.matmul(p_ps[:, pp, :, :], a, b, start=n == 0, stop=n == len(terms) - 1)
                last.then_inc(gram_done, 1)

            def transpose_p(g, q):
                d = 2 * g + q
                pe.wait_ge(p_copied, d + 1)
                if q:
                    pe.wait_ge(s2_done, d)
                for pp in range(2):
                    for s in (L, G):
                        last = pe.transpose(pt_ps[:, pp, s, :], P_sb[q][:, pp, s, :], ident[:, :])
                last.then_inc(pt_done, 1)
                pe.wait_ge(cols_ready, d + 1)
                if q:
                    pe.wait_ge(x0_done, d)
                for s, col in ((L, norms[q][:, 1, :]), (G, sq[q][:, G, :])):
                    for pp in range(2):
                        last = pe.transpose(row_ps[:, s, pp, :], col[:, pp:pp + 1].to_broadcast([R, R]), ident[:, :])
                last.then_inc(rows_done, 1)

            def transpose_k(g, q):
                pe.wait_ge(k_done, 2 * g + q + 1)
                pe.wait_ge(s2_done, 2 * g + 2)
                if q:
                    pe.wait_ge(kt_split, 2 * g + 1)
                for pp in range(2):
                    last = pe.transpose(kt_ps[:, pp, :], K_sb[:, pp, :], ident[:, :])
                last.then_inc(kt_done, 1)

            def apply_k(g, p):
                pe.wait_ge(kt_split, 2 * g + p // 2 + 1)
                pe.wait_ge(proj_split, NPROJ * g + 2 * DC + p + 1)
                if p == 1:
                    pe.wait_ge(x0_done, 2 * g + 2)
                elif p >= 2:
                    pe.wait_ge(z_added, NP * g + p - 1)
                bank = (bank_k, bank_r)[p % 2]
                for n, (a, b) in enumerate(parts(KT_hi, KT_lo, u_hi, u_lo)):
                    last = pe.matmul(bank[:, :], a[:, p % 2, :], b[:, p, :], start=n == 0, stop=n == 2)
                last.then_inc(ku_done, 1)

            def step(g, par, tail=True):
                project(g, par, 0)
                if tail:
                    transpose_p(g - 1, 0)
                project(g, par, 1)
                project(g, par, 2)
                project(g, par, 3)
                if tail:
                    transpose_p(g - 1, 1)
                project(g, par, 4)
                if tail:
                    transpose_k(g - 1, 0)
                project(g, par, 5)
                project(g, par, 6)
                if tail:
                    apply_k(g - 1, 0)
                    apply_k(g - 1, 1)
                project(g, par, 7)
                if tail:
                    transpose_k(g - 1, 1)
                layer0(g + 1, 0)
                layer0(g + 1, 1)
                project(g, par, 8)
                if tail:
                    apply_k(g - 1, 2)
                    apply_k(g - 1, 3)
                layer0(g + 1, 2)
                layer0(g + 1, 3)
                project(g, par, 9)
                project(g, par, 10)
                gram(g, par, 0)
                transpose_h(g + 1, 1 - par, 0)
                transpose_h(g + 1, 1 - par, 1)
                project(g, par, 11)
                transpose_h(g + 1, 1 - par, 2)
                transpose_h(g + 1, 1 - par, 3)
                gram(g, par, 1)

            at = 0

            def setup(cols, terms, split_before=None):
                nonlocal at
                if at >= NRING:
                    pe.wait_ge(setup_split, at - NRING + 1)
                for n, (a, b) in enumerate(terms):
                    if split_before is not None and n % 3 == 0:
                        pe.wait_ge(w_lo_done, split_before + n // 3 + 1)
                    last = pe.matmul(ring[at % NRING][:, 0:cols], a, b, start=n == 0, stop=n == len(terms) - 1)
                last.then_inc(setup_done, 1)
                at += 1

            pe.wait_ge(mix_steps, 6)
            for s in (L, G):
                layer0(0, 2 * s)
                layer0(0, 2 * s + 1)
                for i in range(DC):
                    setup(D - i * R, [(a[:, e, i * R:(i + 1) * R], b[:, e, i * R:D]) for e in range(DC)
                                      for a, b in parts(W_hi[s], W_lo[s], W_hi[s], W_lo[s])],
                          DC * s if i == 0 else None)
            pe.wait_ge(w_loaded[3], 16)
            for e in range(DC):
                pe.wait_ge(setup_split, at - NRING + 1)
                for f in range(DC):
                    last = pe.transpose(ring[at % NRING][:, f * R:(f + 1) * R],
                                        w_raw[0][:, f, e * R:(e + 1) * R], ident[:, :])
                last.then_inc(setup_done, 1)
                at += 1
                transpose_h(0, 0, e)
            pe.wait_ge(w_lo_done, 3 * DC)
            pe.wait_ge(setup_split, at)
            for i in range(DC):
                setup(D, [(a[:, e, i * R:(i + 1) * R], b[:, e, :]) for e in range(DC)
                          for a, b in parts(W_hi[2], W_lo[2], W_hi[3], W_lo[3])])

            step(0, 0, tail=False)
            step(1, 1)
            with pe.Fori(2, NG - 2, 2) as g:
                step(g, 0)
                step(g + 1, 1)
            step(NG - 2, 0)
            g = NG - 1
            project(g, 1, 0)
            transpose_p(g - 1, 0)
            project(g, 1, 1)
            project(g, 1, 2)
            project(g, 1, 3)
            transpose_p(g - 1, 1)
            project(g, 1, 4)
            transpose_k(g - 1, 0)
            project(g, 1, 5)
            project(g, 1, 6)
            apply_k(g - 1, 0)
            apply_k(g - 1, 1)
            project(g, 1, 7)
            transpose_k(g - 1, 1)
            project(g, 1, 8)
            gram(g, 1, 0)
            apply_k(g - 1, 2)
            apply_k(g - 1, 3)
            gram(g, 1, 1)
            pe.wait_ge(kt_split, 2 * g)
            pe.wait_ge(z_added, NP * g)
            transpose_p(g, 0)
            project(g, 1, 9)
            project(g, 1, 10)
            transpose_p(g, 1)
            project(g, 1, 11)
            transpose_k(g, 0)
            apply_k(g, 0)
            apply_k(g, 1)
            transpose_k(g, 1)
            apply_k(g, 2)
            apply_k(g, 3)

        def proj_dst(k, which):
            kind, j = PROJ[k]
            if kind == "u":
                return (u_hi, u_lo)[which][:, j, :]
            return (yT_hi, yT_lo)[which][:, j, kind, :]

        @block.scalar
        def _(act):
            def copy(dst, src, scale=1.0):
                return act.activation(dst, src, ACT.Copy, scale=scale)

            def split_x(g, c):
                if isinstance(g, int) and g == 0:
                    act.wait_ge(x0_loaded[c], 16)
                elif c == 0:
                    act.wait_ge(x_loaded, 16 * g)
                    act.wait_ge(l0_done, NP * g)
                s = slice(2 * c, 2 * c + 2)
                copy(x_hi[:, s, :], x_sb[:, s, :]).then_inc(x_hi_done, 1)

            def normalise_h(g, par, p):
                act.wait_ge(y_scale, 2 * g + p // 2 + 1)
                act.activation(h_sb[par][:, p, :], h_sb[par][:, p, :], ACT.Identity, scale=y_rs[:, p:p + 1],
                               bias=y_nb[:, p:p + 1]).then_inc(h_ready, 1)

            def hi_hT(g, par, p):
                act.wait_ge(hT_done, NP * g + p + 1)
                copy(hT_hi[par][:, :, p * R:(p + 1) * R],
                     hT_banks[p][:, :].rearrange("p (c r) -> p c r", c=DC)).then_inc(hT_hi_done, 1)

            def hi_proj(g, k):
                act.wait_ge(proj_done, NPROJ * g + k + 1)
                copy(proj_dst(k, 0), ring[ring_of(k)][:, :]).then_inc(proj_hi, 1)

            def copy_p(g, q):
                act.wait_ge(gram_done, 2 * g + q + 1)
                if not (isinstance(g, int) and g == 0):
                    act.wait_ge(s2_done, 2 * g + q - 1)
                copy(P_sb[q][:, :, :, :], p_ps).then_inc(p_copied, 1)

            def exp_g(g, q):
                act.wait_ge(negd_done, 2 * g + q + 1)
                for pp in range(2):
                    last = act.activation(E_g[:, pp, :], negd[:, pp, :], ACT.Exp, scale=neg_inv[:, 0:1],
                                          bias=exp_bias[q][:, pp:pp + 1])
                last.then_inc(exp_done, 1)

            def scale_l(g, q):
                act.wait_ge(coef_done, 2 * g + q + 1)
                for pp in range(2):
                    last = act.activation(K_l[:, pp, :], X_l[:, pp, :], ACT.Copy, scale=coef[:, pp:pp + 1])
                last.then_inc(kl_done, 1)

            def hi_kt(g, q):
                act.wait_ge(kt_done, 2 * g + q + 1)
                copy(KT_hi[:, :, :], kt_ps).then_inc(kt_hi_done, 1)

            def normalise_out(g, p):
                act.wait_ge(z_scale, 2 * g + p // 2 + 1)
                act.activation(o_sb[:, p, :], o_sb[:, p, :], ACT.Identity, scale=z_rs[:, p:p + 1],
                               bias=z_nb[:, p:p + 1]).then_inc(o_ready, 1)

            def step(g, par, tail=True):
                split_x(g + 1, 0)
                split_x(g + 1, 1)
                hi_proj(g, 0)
                hi_proj(g, 1)
                if tail:
                    exp_g(g - 1, 0)
                hi_proj(g, 2)
                if tail:
                    scale_l(g - 1, 0)
                hi_proj(g, 3)
                if tail:
                    exp_g(g - 1, 1)
                hi_proj(g, 4)
                if tail:
                    hi_kt(g - 1, 0)
                    scale_l(g - 1, 1)
                hi_proj(g, 5)
                hi_proj(g, 6)
                hi_proj(g, 7)
                if tail:
                    hi_kt(g - 1, 1)
                    normalise_out(g - 1, 0)
                    normalise_out(g - 1, 1)
                hi_proj(g, 8)
                normalise_h(g + 1, 1 - par, 0)
                normalise_h(g + 1, 1 - par, 1)
                if tail:
                    normalise_out(g - 1, 2)
                hi_proj(g, 9)
                if tail:
                    normalise_out(g - 1, 3)
                hi_proj(g, 10)
                copy_p(g, 0)
                normalise_h(g + 1, 1 - par, 2)
                normalise_h(g + 1, 1 - par, 3)
                hi_hT(g + 1, 1 - par, 0)
                hi_hT(g + 1, 1 - par, 1)
                hi_proj(g, 11)
                hi_hT(g + 1, 1 - par, 2)
                hi_hT(g + 1, 1 - par, 3)
                copy_p(g, 1)

            def hi_weight(i):
                act.wait_ge(w_loaded[i], 16)
                for c in range(DC):
                    copy(W_hi[i][:, c, :], w_raw[i][:, c, :]).then_inc(w_hi_done, 1)

            def hi_row(s, i):
                at = DC * s + i
                act.wait_ge(setup_done, at + 1)
                bank = ring[at % NRING]
                last = copy(T_hi[s][:, ROW_AT[i], :], bank[:, 0:R])
                if i < DC - 1:
                    last = copy(T_hi[s][:, ROW_AT[i] + 1:ROW_AT[i] + DC - i, :],
                                bank[:, R:D - i * R].rearrange("p (b c) -> p b c", c=R), scale=2.0)
                last.then_inc(setup_hi, 1)

            act.wait_ge(mix_steps, 4)
            copy(mix_hi[:, :], mix[:, :]).then_inc(mix_steps, 1)
            split_x(0, 0)
            split_x(0, 1)
            hi_weight(0)
            act.wait_ge(gates_loaded, 32)
            act.activation(gate_e[:, 0:1], gates[:, 0:1], ACT.Exp, scale=-1.0)
            act.activation(gate_e[:, 1:2], gates[:, 1:2], ACT.Exp).then_inc(gate_exp, 1)
            hi_weight(1)
            for i in range(DC):
                hi_row(L, i)
            normalise_h(0, 0, 0)
            normalise_h(0, 0, 1)
            hi_weight(2)
            for i in range(DC):
                hi_row(G, i)
            normalise_h(0, 0, 2)
            normalise_h(0, 0, 3)
            for dst in (W_hi[3], M_hi[:, :, :]):
                for i in range(DC):
                    at = (2 if dst is W_hi[3] else 3) * DC + i
                    act.wait_ge(setup_done, at + 1)
                    copy(dst[:, i, :], ring[at % NRING][:, :]).then_inc(setup_hi, 1)
                    if dst is W_hi[3]:
                        hi_hT(0, 0, i)

            step(0, 0, tail=False)
            step(1, 1)
            with act.Fori(2, NG - 2, 2) as g:
                step(g, 0)
                step(g + 1, 1)
            step(NG - 2, 0)
            g = NG - 1
            hi_proj(g, 0)
            hi_proj(g, 1)
            exp_g(g - 1, 0)
            hi_proj(g, 2)
            scale_l(g - 1, 0)
            hi_proj(g, 3)
            exp_g(g - 1, 1)
            hi_proj(g, 4)
            hi_kt(g - 1, 0)
            scale_l(g - 1, 1)
            hi_proj(g, 5)
            hi_proj(g, 6)
            hi_proj(g, 7)
            hi_kt(g - 1, 1)
            normalise_out(g - 1, 0)
            normalise_out(g - 1, 1)
            copy_p(g, 0)
            hi_proj(g, 8)
            copy_p(g, 1)
            exp_g(g, 0)
            normalise_out(g - 1, 2)
            hi_proj(g, 9)
            scale_l(g, 0)
            normalise_out(g - 1, 3)
            hi_proj(g, 10)
            exp_g(g, 1)
            scale_l(g, 1)
            hi_proj(g, 11)
            hi_kt(g, 0)
            hi_kt(g, 1)
            for p in range(NP):
                normalise_out(g, p)

        @block.vector
        def _(dve):
            def add_y(g, par, q):
                duo = (2 * q, 2 * q + 1)
                for p in duo:
                    dve.wait_ge(l0_done, NP * g + p + 1)
                    dve.tensor_tensor(h_sb[par][:, p, :], (bank_x, bank_p)[p % 2][:, :], bias_bc[:, :],
                                      ALU.add).then_inc(y_added, 1)
                for p in duo:
                    dve.wait_ge(y_added, NP * g + p + 1)
                    dve.bn_stats(y_bn[:, p, :], h_sb[par][:, p, :]).then_inc(y_counted, 1)
                dve.wait_ge(y_counted, NP * g + 2 * q + 2)
                settle(dve)
                for p in duo:
                    last = dve.bn_aggr(y_mv[:, p, :], y_bn[:, p, :])
                last.then_inc(y_stats, 1)

            def lo_hT(g, par, p):
                dve.wait_ge(hT_hi_done, NP * g + p + 1)
                s = slice(p * R, (p + 1) * R)
                dve.tensor_tensor(hT_lo[par][:, :, s], hT_banks[p][:, :].rearrange("p (c r) -> p c r", c=DC),
                                  hT_hi[par][:, :, s], ALU.subtract).then_inc(hT_split, 1)

            def lo_proj(g, k):
                dve.wait_ge(proj_hi, NPROJ * g + k + 1)
                dve.tensor_tensor(proj_dst(k, 1), ring[ring_of(k)][:, :], proj_dst(k, 0),
                                  ALU.subtract).then_inc(proj_split, 1)

            def diagonals(g, q):
                dve.wait_ge(p_copied, 2 * g + q + 1)
                if q:
                    dve.wait_ge(sq_done, 2 * g + q)
                for pp in range(2):
                    for s in (L, G):
                        last = dve.tensor_tensor_reduce(
                            out=diag_scr[:, 2 * pp + s, :], in0=P_sb[q][:, pp, s, :], in1=ident[:, :], scale=1.0,
                            scalar=0.0, op0=ALU.mult, op1=ALU.add, accum_out=sq[q][:, s, pp:pp + 1])
                last.then_inc(sq_done, 1)

            def similarities(g, q):
                d = 2 * g + q
                dve.wait_ge(pt_done, d + 1)
                dve.tensor_tensor(S2[:, :, :, :], pt_ps, P_sb[q][:, :, :, :], ALU.add).then_inc(s2_done, 1)
                dve.wait_ge(rows_done, d + 1)
                dve.wait_ge(s2_done, d + 1)
                dve.scalar_tensor_tensor(negd[:, :, :], S2[:, :, G, :], -1.0, row_ps[:, G, :, :], ALU.mult,
                                         ALU.add).then_inc(negd_done, 1)
                dve.scalar_tensor_tensor(X0[:, :, :], S2[:, :, L, :], 0.0, row_ps[:, L, :, :], ALU.max,
                                         ALU.mult).then_inc(x0_done, 1)
                dve.wait_ge(x0_done, d + 1)
                for pp in range(2):
                    last = dve.tensor_tensor_reduce(
                        out=X_l[:, pp, :], in0=X0[:, pp, :], in1=mask[:, :], scale=1.0, scalar=0.0,
                        op0=ALU.mult, op1=ALU.add, accum_out=sums[:, pp:pp + 1])
                last.then_inc(xl_done, 1)

            def coefficients(g, q):
                d = 2 * g + q
                dve.wait_ge(exp_done, d + 1)
                for pp in range(2):
                    last = dve.scalar_tensor_tensor(X_g[:, pp, :], E_g[:, pp, :], 1.0, mask[:, :], ALU.min, ALU.mult,
                                                    accum_out=sums[:, 2 + pp:3 + pp])
                last.then_inc(xg_done, 1)
                dve.wait_ge(xg_done, d + 1)
                dve.wait_ge(xl_done, d + 1)
                dve.tensor_tensor(dens[:, :], sums[:, :], floors[q][:, :], ALU.max).then_inc(dens_done, 1)
                dve.wait_ge(dens_done, d + 1)
                dve.reciprocal(recs[:, :], dens[:, :]).then_inc(recs_done, 1)
                dve.wait_ge(recs_done, d + 1)
                dve.tensor_tensor(coef[:, :], recs[:, :], mixw[:, :], ALU.mult).then_inc(coef_done, 1)

            def combine(g, q):
                dve.wait_ge(coef_done, 2 * g + q + 1)
                dve.wait_ge(kl_done, 2 * g + q + 1)
                for pp in range(2):
                    last = dve.scalar_tensor_tensor(K_sb[:, pp, :], X_g[:, pp, :], coef[:, 2 + pp:3 + pp],
                                                    K_l[:, pp, :], ALU.mult, ALU.add)
                last.then_inc(k_done, 1)

            def lo_kt(g, q):
                dve.wait_ge(kt_hi_done, 2 * g + q + 1)
                dve.tensor_tensor(KT_lo[:, :, :], kt_ps, KT_hi[:, :, :], ALU.subtract).then_inc(kt_split, 1)

            def add_z(g, par, q):
                duo = (2 * q, 2 * q + 1)
                for p in duo:
                    dve.wait_ge(ku_done, NP * g + p + 1)
                    if not (isinstance(g, int) and g == 0):
                        dve.wait_ge(stored[p], 16 * g)
                    dve.tensor_tensor(o_sb[:, p, :], (bank_k, bank_r)[p % 2][:, :], h_sb[par][:, p, :],
                                      ALU.add).then_inc(z_added, 1)
                for p in duo:
                    dve.wait_ge(z_added, NP * g + p + 1)
                    dve.bn_stats(z_bn[:, p, :], o_sb[:, p, :]).then_inc(z_counted, 1)
                dve.wait_ge(z_counted, NP * g + 2 * q + 2)
                settle(dve)
                for p in duo:
                    last = dve.bn_aggr(z_mv[:, p, :], z_bn[:, p, :])
                last.then_inc(z_stats, 1)

            def step(g, par, tail=True):
                if tail:
                    diagonals(g - 1, 1)
                lo_proj(g, 0)
                if tail:
                    similarities(g - 1, 0)
                lo_proj(g, 1)
                if tail:
                    coefficients(g - 1, 0)
                lo_proj(g, 2)
                if tail:
                    combine(g - 1, 0)
                lo_proj(g, 3)
                if tail:
                    similarities(g - 1, 1)
                    coefficients(g - 1, 1)
                    lo_kt(g - 1, 0)
                lo_proj(g, 4)
                if tail:
                    combine(g - 1, 1)
                lo_proj(g, 5)
                lo_proj(g, 6)
                if tail:
                    add_z(g - 1, 1 - par, 0)
                lo_proj(g, 7)
                if tail:
                    lo_kt(g - 1, 1)
                add_y(g + 1, 1 - par, 0)
                lo_proj(g, 8)
                if tail:
                    add_z(g - 1, 1 - par, 1)
                add_y(g + 1, 1 - par, 1)
                lo_proj(g, 9)
                lo_proj(g, 10)
                diagonals(g, 0)
                lo_hT(g + 1, 1 - par, 0)
                lo_hT(g + 1, 1 - par, 1)
                lo_proj(g, 11)
                lo_hT(g + 1, 1 - par, 2)
                lo_hT(g + 1, 1 - par, 3)

            dve.wait_ge(ident_ready, 2)
            dve.tensor_scalar(off_diag[:, :], ident[:, :], -1.0, 1.0, ALU.mult, ALU.add).then_inc(mix_steps, 1)
            dve.wait_ge(adj_loaded, 32)
            dve.tensor_tensor(mix[:, :], adj_bd[:, :], adj_bd[:, :], ALU.mult).then_inc(mix_steps, 1)
            dve.wait_ge(mix_steps, 2)
            dve.tensor_tensor(mix[:, :], mix[:, :], ident[:, :], ALU.add).then_inc(mix_steps, 1)
            dve.tensor_tensor(mask[:, :], adj_bd[:, :], off_diag[:, :], ALU.mult).then_inc(mix_steps, 1)
            dve.wait_ge(mix_steps, 5)
            dve.tensor_tensor(mix_lo[:, :], mix[:, :], mix_hi[:, :], ALU.subtract).then_inc(mix_steps, 1)

            def lo_weight(i):
                for c in range(DC):
                    dve.wait_ge(w_hi_done, DC * i + c + 1)
                    dve.tensor_tensor(W_lo[i][:, c, :], w_raw[i][:, c, :], W_hi[i][:, c, :],
                                      ALU.subtract).then_inc(w_lo_done, 1)

            def lo_row(s, i):
                at = DC * s + i
                dve.wait_ge(setup_hi, at + 1)
                bank = ring[at % NRING]
                first = ROW_AT[i]
                last = dve.tensor_tensor(T_lo[s][:, first, :], bank[:, 0:R], T_hi[s][:, first, :], ALU.subtract)
                if i < DC - 1:
                    b = slice(first + 1, first + DC - i)
                    last = dve.scalar_tensor_tensor(
                        T_lo[s][:, b, :], bank[:, R:D - i * R].rearrange("p (b c) -> p b c", c=R), 2.0,
                        T_hi[s][:, b, :], ALU.mult, ALU.subtract)
                last.then_inc(setup_split, 1)

            lo_weight(0)
            dve.wait_ge(bias_loaded, 16)
            add_y(0, 0, 0)
            lo_weight(1)
            for i in range(DC):
                lo_row(L, i)
            dve.wait_ge(gate_exp, 1)
            dve.tensor_scalar(gate_t[:, 0:1], gate_e[:, 0:1], 1.0, None, ALU.add)
            dve.scalar_tensor_tensor(gate_t[:, 1:2], gate_e[:, 1:2], -2.0, gate_e[:, 1:2], ALU.mult,
                                     ALU.mult).then_inc(gate_steps, 1)
            dve.wait_ge(gate_steps, 1)
            dve.reciprocal(gate_t[:, 2:4], gate_t[:, 0:2]).then_inc(gate_steps, 1)
            dve.wait_ge(gate_steps, 2)
            dve.tensor_copy(neg_inv[:, :], gate_t[:, 3:4])
            dve.tensor_copy(mixw[:, 0:2], gate_t[:, 2:3].to_broadcast([R, 2]))
            dve.tensor_scalar(mixw[:, 2:4], gate_t[:, 2:3].to_broadcast([R, 2]), -1.0, 1.0, ALU.mult,
                              ALU.add).then_inc(gate_steps, 1)
            dve.wait_ge(gate_steps, 3)
            add_y(0, 0, 1)
            lo_weight(2)
            for i in range(DC):
                lo_row(G, i)
            for hi, lo in ((W_hi[3], W_lo[3]), (M_hi[:, :, :], M_lo[:, :, :])):
                for i in range(DC):
                    at = (2 if hi is W_hi[3] else 3) * DC + i
                    dve.wait_ge(setup_hi, at + 1)
                    dve.tensor_tensor(lo[:, i, :], ring[at % NRING][:, :], hi[:, i, :],
                                      ALU.subtract).then_inc(setup_split, 1)
                    if hi is W_hi[3]:
                        lo_hT(0, 0, i)

            step(0, 0, tail=False)
            step(1, 1)
            with dve.Fori(2, NG - 2, 2) as g:
                step(g, 0)
                step(g + 1, 1)
            step(NG - 2, 0)
            g = NG - 1
            diagonals(g - 1, 1)
            lo_proj(g, 0)
            similarities(g - 1, 0)
            lo_proj(g, 1)
            coefficients(g - 1, 0)
            lo_proj(g, 2)
            combine(g - 1, 0)
            lo_proj(g, 3)
            similarities(g - 1, 1)
            coefficients(g - 1, 1)
            lo_kt(g - 1, 0)
            lo_proj(g, 4)
            combine(g - 1, 1)
            lo_proj(g, 5)
            lo_proj(g, 6)
            add_z(g - 1, 0, 0)
            lo_proj(g, 7)
            lo_kt(g - 1, 1)
            diagonals(g, 0)
            add_z(g - 1, 0, 1)
            lo_proj(g, 8)
            similarities(g, 0)
            diagonals(g, 1)
            coefficients(g, 0)
            lo_proj(g, 9)
            combine(g, 0)
            lo_proj(g, 10)
            similarities(g, 1)
            coefficients(g, 1)
            lo_proj(g, 11)
            lo_kt(g, 0)
            combine(g, 1)
            add_z(g, 1, 0)
            lo_kt(g, 1)
            add_z(g, 1, 1)

        @block.gpsimd
        def _(pool):
            def split_x(g, p):
                pool.wait_ge(x_hi_done, 2 * g + p // 2 + 1)
                pool.tensor_tensor(x_lo[:, p, :], x_sb[:, p, :], x_hi[:, p, :], ALU.subtract).then_inc(x_lo_done, 1)

            def scale_of(stats, ve_done, rs_done, scale, mv, ve, nm, rs, nb, d, q):
                pq = slice(2 * q, 2 * q + 2)
                pool.wait_ge(stats, d + 1)
                settle(pool)
                pool.tensor_scalar(ve[:, pq], mv[:, pq, 1], LN_EPS, None, ALU.add).then_inc(ve_done, 1)
                pool.wait_ge(ve_done, d + 1)
                pool.tensor_tensor(rs[:, pq], ve[:, pq], pow_half[:, 2:4], ALU.pow).then_inc(rs_done, 1)
                pool.tensor_scalar(nm[:, pq], mv[:, pq, 0], -1.0, None, ALU.mult).then_inc(rs_done, 1)
                pool.wait_ge(rs_done, 2 * d + 2)
                pool.tensor_tensor(nb[:, pq], nm[:, pq], rs[:, pq], ALU.mult).then_inc(scale, 1)

            def scale_y(g, q):
                scale_of(y_stats, y_ve_done, y_rs_done, y_scale, y_mv, y_ve, y_nm, y_rs, y_nb, 2 * g + q, q)

            def scale_z(g, q):
                scale_of(z_stats, z_ve_done, z_rs_done, z_scale, z_mv, z_ve, z_nm, z_rs, z_nb, 2 * g + q, q)

            def columns(g, q):
                d = 2 * g + q
                pool.wait_ge(sq_done, d + 1)
                settle(pool)
                for c in range(2):
                    last = pool.tensor_scalar(sq_floor[q][:, c, :], sq[q][:, L, :], EPS * EPS, None, ALU.max)
                last.then_inc(floor_done, 1)
                pool.tensor_scalar(exp_bias[q][:, :], sq[q][:, G, :], neg_inv[:, 0:1], None, ALU.mult)
                pool.wait_ge(floor_done, d + 1)
                pool.tensor_tensor(norms[q][:, :, :], sq_floor[q][:, :, :],
                                   pow_half[:, :].rearrange("r (a b) -> r a b", a=2), ALU.pow).then_inc(norm_done, 1)
                pool.wait_ge(norm_done, d + 1)
                settle(pool)
                pool.tensor_scalar(floors[q][:, 0:2], norms[q][:, 0, :], 2 * EPS, None, ALU.mult).then_inc(cols_ready, 1)

            def step(g, tail=True):
                if tail:
                    columns(g - 1, 1)
                for p in range(NP):
                    split_x(g + 1, p)
                for q in range(2):
                    if tail:
                        scale_z(g - 1, q)
                    scale_y(g + 1, q)
                columns(g, 0)

            pool.memset(adj_bd[:, :], 0.0).then_inc(adj_zeroed, 1)
            pool.memset(ident[:, :], 0.0).then_inc(ident_ready, 1)
            pool.wait_ge(ident_ready, 1)
            pool.affine_select(out=ident[:, :], in_=ident[:, :], compare_op=ALU.not_equal, fill=1.0, base=0,
                               pattern=[[-1, R]], channel_multiplier=1).then_inc(ident_ready, 1)
            pool.memset(pow_half[:, 0:2], 0.5)
            pool.memset(pow_half[:, 2:4], -0.5)
            pool.memset(floors[0][:, 2:4], EPS)
            pool.memset(floors[1][:, 2:4], EPS).then_inc(pow_ready, 1)
            pool.wait_ge(pow_ready, 1)
            for p in range(NP):
                split_x(0, p)
            for q in range(2):
                scale_y(0, q)
            pool.wait_ge(gate_steps, 3)

            step(0, tail=False)
            step(1)
            with pool.Fori(2, NG - 2, 1) as g:
                step(g)
            step(NG - 2)
            g = NG - 1
            columns(g - 1, 1)
            scale_z(g - 1, 0)
            columns(g, 0)
            scale_z(g - 1, 1)
            columns(g, 1)
            for q in range(2):
                scale_z(g, q)


_INS = ['x', 'adj', 'L0_gnn_bias', 'L1_gnn_W_lang', 'L1_gnn_W_grav', 'L1_gnn_W_V', 'L1_gnn_W_O', 'L1_gnn_gate_logit',
        'L1_gnn_log_sigma']
_OUTS = [((128, 64, 512), 'float32')]


def kernel(**inputs):
    import numpy as _np
    import concourse.bacc as _bacc
    from concourse import mybir as _mybir
    from concourse.bass_utils import run_bass_kernel_spmd as _run

    nc = _bacc.Bacc("TRN2", target_bir_lowering=False, num_devices=1)
    arrays, args = {}, []
    for name in _INS:
        a = _np.ascontiguousarray(inputs[name])
        arrays[f"in_{name}_dram"] = a
        args.append(nc.dram_tensor(f"in_{name}_dram", a.shape, _mybir.dt.from_np(a.dtype), kind="ExternalInput").ap())
    for i, (shape, dtype) in enumerate(_OUTS):
        dt = _mybir.dt.from_np(_np.dtype(dtype))
        args.append(nc.dram_tensor(f"out_{i}_dram", shape, dt, kind="ExternalOutput").ap())
    bass_two_layer_graph_resnorm(nc, *args)
    r = _run(nc, [arrays], core_ids=[0])
    got = tuple(r.results[0][f"out_{i}_dram"] for i in range(len(_OUTS)))
    return got[0]
```

```python
import concourse.bass as bass
from concourse import mybir
from contextlib import ExitStack


def bass_two_layer_graph_resnorm(
    nc: bass.Bass,
    x: bass.AP,
    adj: bass.AP,
    bias: bass.AP,
    w_lang: bass.AP,
    w_grav: bass.AP,
    w_v: bass.AP,
    w_o: bass.AP,
    gate_logit: bass.AP,
    log_sigma: bass.AP,
    out: bass.AP,
):
    fp32 = mybir.dt.float32
    fp32r = mybir.dt.float32r
    ALU = mybir.AluOpType
    ACT = mybir.ActivationFunctionType

    B, N, D = x.shape
    R = 128
    NP = 4
    NG = B * N // (R * NP)
    DC = D // R
    GT = NP * R
    LN_EPS = 1e-5
    EPS = 1e-8
    L, G = 0, 1
    NBLK = DC * (DC + 1) // 2
    ROW_AT = [i * DC - i * (i - 1) // 2 for i in range(DC)]
    PROJ = [(L, 3), (L, 0), (L, 2), (L, 1), (G, 3), (G, 0), (G, 2), (G, 1)] + [("u", p) for p in range(NP)]
    NPROJ = len(PROJ)
    WARM_UP = 27
    NRING = 3
    NSETUP = 2 * DC + 2 * DC
    assert NG % 2 == 0 and NPROJ % NRING == 0

    def ring_of(k):
        return (NSETUP + k) % NRING

    x_v = x.rearrange("(g p b) n f -> g (b n) p f", p=NP, b=2)
    out_v = out.rearrange("(g p b) n f -> g (b n) p f", p=NP, b=2)

    ctx = ExitStack()
    with ctx:
        def sb(name, shape, dt=fp32):
            return ctx.enter_context(nc.sbuf_tensor(name, shape, dt))

        def pb(name):
            return ctx.enter_context(nc.psum_tensor(name, [R, 512], fp32))

        def sem(name):
            return ctx.enter_context(nc.semaphore(name))

        ident = sb("ident", [R, R])
        off_diag = sb("off_diag", [R, R])
        adj_bd = sb("adj_bd", [R, R])
        mask = sb("mask", [R, R])
        mix = sb("mix", [R, R])
        mix_hi = sb("mix_hi", [R, R], fp32r)
        mix_lo = sb("mix_lo", [R, R], fp32r)
        bias_bc = sb("bias_bc", [R, D])
        gates = sb("gates", [R, 2])
        gate_e = sb("gate_e", [R, 2])
        gate_t = sb("gate_t", [R, 4])
        inv_2s2 = sb("inv_2s2", [R, 1])
        mixw = sb("mixw", [R, 4])
        pow_neg_half = sb("pow_neg_half", [R, 2])
        T_hi = [sb(f"T_hi{s}", [R, NBLK, R], fp32r) for s in (L, G)]
        T_lo = [sb(f"T_lo{s}", [R, NBLK, R], fp32r) for s in (L, G)]
        M_hi = sb("M_hi", [R, DC, D], fp32r)
        M_lo = sb("M_lo", [R, DC, D], fp32r)
        x_sb = sb("x_sb", [R, NP, D])
        x_hi = sb("x_hi", [R, NP, D], fp32r)
        x_lo = sb("x_lo", [R, NP, D], fp32r)
        h_sb = [sb(f"h_sb{i}", [R, NP, D]) for i in range(2)]
        hT_hi = [sb(f"hT_hi{i}", [R, DC, GT], fp32r) for i in range(2)]
        hT_lo = [sb(f"hT_lo{i}", [R, DC, GT], fp32r) for i in range(2)]
        yT_hi = sb("yT_hi", [R, DC, 2, GT], fp32r)
        yT_lo = sb("yT_lo", [R, DC, 2, GT], fp32r)
        u_hi = sb("u_hi", [R, NP, D], fp32r)
        u_lo = sb("u_lo", [R, NP, D], fp32r)
        P_sb = [sb(f"P_sb{q}", [R, 2, 2, R]) for q in range(2)]
        diag_scr = sb("diag_scr", [R, 4, R])
        S2 = sb("S2", [R, 2, 2, R])
        X0 = sb("X0", [R, 2, R])
        X_l = sb("X_l", [R, 2, R])
        E_g = sb("E_g", [R, 2, R])
        X_g = sb("X_g", [R, 2, R])
        K_l = sb("K_l", [R, 2, R])
        K_sb = sb("K_sb", [R, 2, R])
        KT_hi = [sb(f"KT_hi{q}", [R, 2, R], fp32r) for q in range(2)]
        KT_lo = [sb(f"KT_lo{q}", [R, 2, R], fp32r) for q in range(2)]
        sq = [sb(f"sq{q}", [R, 2, 2]) for q in range(2)]
        sq_floor = [sb(f"sq_floor{q}", [R, 2]) for q in range(2)]
        inv_norm = [sb(f"inv_norm{q}", [R, 2]) for q in range(2)]
        sq_eps = [sb(f"sq_eps{q}", [R, 2]) for q in range(2)]
        floors = [sb(f"floors{q}", [R, 4]) for q in range(2)]
        sums = sb("sums", [R, 4])
        dens = sb("dens", [R, 4])
        recs = sb("recs", [R, 4])
        coef = sb("coef", [R, 4])
        y_bn = sb("y_bn", [R, NP, 6])
        y_mv = sb("y_mv", [R, NP, 2])
        y_ve = sb("y_ve", [R, NP])
        y_nm = sb("y_nm", [R, NP])
        y_rs = sb("y_rs", [R, NP])
        y_nb = sb("y_nb", [R, NP])
        z_bn = sb("z_bn", [R, NP, 6])
        z_mv = sb("z_mv", [R, NP, 2])
        z_ve = sb("z_ve", [R, NP])
        z_nm = sb("z_nm", [R, NP])
        z_rs = sb("z_rs", [R, NP])
        z_nb = sb("z_nb", [R, NP])
        o_sb = sb("o_sb", [R, NP, D])
        w_raw = [sb("w_raw", [R, DC, D]), o_sb, h_sb[1]]
        yT_w = [t[:, :, :, :].rearrange("p a s t -> p (a s t)") for t in (yT_hi, yT_lo)]

        def half(view, k):
            return view[:, k * DC * D:(k + 1) * DC * D].rearrange("p (c d) -> p c d", c=DC)

        W_hi = [half(yT_w[0], 0), half(yT_w[0], 1), u_hi[:, :, :], hT_hi[1][:, :, :]]
        W_lo = [half(yT_w[1], 0), half(yT_w[1], 1), u_lo[:, :, :], hT_lo[1][:, :, :]]

        ring = [pb(f"ring{i}") for i in range(NRING)]
        bank_x = pb("bank_x")
        bank_k = pb("bank_k")
        bank_p = pb("bank_p")
        bank_pt = pb("bank_pt")
        bank_r = pb("bank_r")
        hT_banks = [bank_x, bank_k, bank_pt, bank_r]
        p_ps = bank_p[:, :].rearrange("r (p s c) -> r p s c", p=2, s=2)
        last_p_ps = bank_x[:, :].rearrange("r (p s c) -> r p s c", p=2, s=2)
        pt_ps = bank_pt[:, :].rearrange("r (p s c) -> r p s c", p=2, s=2)
        row_ps = bank_r[:, 0:2 * R].rearrange("r (p c) -> r p c", p=2)
        kt_ps = bank_pt[:, 0:2 * R].rearrange("r (p c) -> r p c", p=2)
        last_kt_ps = bank_p[:, 0:2 * R].rearrange("r (p c) -> r p c", p=2)

        w_loaded = [sem(f"w_loaded{i}") for i in range(4)]
        adj_zeroed = sem("adj_zeroed")
        adj_loaded = sem("adj_loaded")
        bias_loaded = sem("bias_loaded")
        gates_loaded = sem("gates_loaded")
        ident_ready = sem("ident_ready")
        pow_ready = sem("pow_ready")
        mix_steps = sem("mix_steps")
        gate_exp = sem("gate_exp")
        gate_steps = sem("gate_steps")
        w_hi_done = sem("w_hi_done")
        w_lo_done = sem("w_lo_done")
        setup_done = sem("setup_done")
        setup_hi = sem("setup_hi")
        setup_split = sem("setup_split")
        x0_loaded = [sem(f"x0_loaded{c}") for c in range(2)]
        x_loaded = sem("x_loaded")
        x0_hi_done = sem("x0_hi_done")
        x_hi_done = sem("x_hi_done")
        x_lo_done = sem("x_lo_done")
        l0_done = sem("l0_done")
        y_added = sem("y_added")
        y_counted = sem("y_counted")
        y_stats = sem("y_stats")
        y_ve_done = sem("y_ve_done")
        y_rs_done = sem("y_rs_done")
        y_scale = sem("y_scale")
        h_ready = sem("h_ready")
        hT_done = sem("hT_done")
        hT_hi_done = sem("hT_hi_done")
        hT_split = sem("hT_split")
        proj_done = sem("proj_done")
        proj_hi = sem("proj_hi")
        proj_split = sem("proj_split")
        gram_done = sem("gram_done")
        p_copied = sem("p_copied")
        sq_done = sem("sq_done")
        floor_done = sem("floor_done")
        sq_eps_done = sem("sq_eps_done")
        floors_ready = sem("floors_ready")
        shift_done = sem("shift_done")
        cols_ready = sem("cols_ready")
        pt_done = sem("pt_done")
        rows_done = sem("rows_done")
        s2_done = sem("s2_done")
        x0_done = sem("x0_done")
        xl_done = sem("xl_done")
        exp_done = sem("exp_done")
        xg_done = sem("xg_done")
        dens_done = sem("dens_done")
        recs_done = sem("recs_done")
        coef_done = sem("coef_done")
        kl_done = sem("kl_done")
        k_done = sem("k_done")
        kt_done = sem("kt_done")
        kt_hi_done = sem("kt_hi_done")
        kt_split = sem("kt_split")
        ku_done = sem("ku_done")
        z_added = sem("z_added")
        z_counted = sem("z_counted")
        z_stats = sem("z_stats")
        z_ve_done = sem("z_ve_done")
        z_rs_done = sem("z_rs_done")
        z_scale = sem("z_scale")
        o_ready = sem("o_ready")
        o_last_ready = sem("o_last_ready")
        stored = [sem(f"stored{p}") for p in range(NP)]

        block = ctx.enter_context(nc.Block())

        def p_bank(g, q):
            return last_p_ps if isinstance(g, int) and g == NG - 1 and q else p_ps

        def out_rows(g):
            return x_sb if isinstance(g, int) and g == NG - 1 else o_sb

        def kt_bank(g):
            return last_kt_ps if isinstance(g, int) and g == NG - 1 else kt_ps

        def parts(hi, lo, hi2, lo2):
            return [(hi, hi2), (hi, lo2), (lo, hi2)]

        def settle(engine):
            engine.nop(nofuse=True)

        @block.sync
        def _(sp):
            sp.dma_start(x_sb[:, 0:2, :], x_v[0][:, 0:2, :]).then_inc(x0_loaded[0], 16)
            sp.wait_ge(adj_zeroed, 1)
            for b in range(2):
                s = slice(b * N, (b + 1) * N)
                sp.dma_start(adj_bd[s, s], adj).then_inc(adj_loaded, 16)
            sp.dma_start(w_raw[0][:, :, :], w_lang.rearrange("(c p) d -> p c d", p=R)).then_inc(w_loaded[0], 16)
            sp.dma_start(bias_bc[:, :], bias.partition_broadcast(R)).then_inc(bias_loaded, 16)
            sp.dma_start(x_sb[:, 2:4, :], x_v[0][:, 2:4, :]).then_inc(x0_loaded[1], 16)
            sp.dma_start(gates[:, 0:1], gate_logit.partition_broadcast(R)).then_inc(gates_loaded, 16)
            sp.dma_start(gates[:, 1:2], log_sigma.partition_broadcast(R)).then_inc(gates_loaded, 16)
            for i, w in ((1, w_grav), (2, w_v)):
                sp.dma_start(w_raw[i][:, :, :], w.rearrange("(c p) d -> p c d", p=R)).then_inc(w_loaded[i], 16)
            sp.wait_ge(w_lo_done, DC)
            sp.dma_start(w_raw[0][:, :, :], w_o.rearrange("(c p) d -> p c d", p=R)).then_inc(w_loaded[3], 16)
            sp.wait_ge(x_lo_done, NP)
            sp.dma_start(x_sb[:, :, :], x_v[1]).then_inc(x_loaded, 16)

            def load(g):
                sp.wait_ge(x_lo_done, NP * g)
                sp.dma_start(x_sb[:, :, :], x_v[g]).then_inc(x_loaded, 16)

            def store(g):
                for p in range(NP):
                    if isinstance(g, int) and g == NG - 1 and p == NP - 1:
                        sp.wait_ge(o_last_ready, 1)
                    else:
                        sp.wait_ge(o_ready, NP * g + p + 1)
                    sp.dma_start(out_v[g][:, p, :], out_rows(g)[:, p, :]).then_inc(stored[p], 16)

            load(2)
            with sp.Fori(1, NG - 2, 1) as g:
                load(g + 2)
                store(g - 1)
            store(NG - 3)
            store(NG - 2)
            store(NG - 1)
            for p in range(NP):
                sp.wait_ge(stored[p], 16 * NG)

        @block.tensor
        def _(pe):
            def layer0(g, p):
                pe.wait_ge(x_lo_done, NP * g + p + 1)
                if p >= 2:
                    pe.wait_ge(y_added, NP * g + p - 1)
                elif p == 1 and not (isinstance(g, int) and g < 2):
                    pe.wait_ge(p_copied, 2 * g - 2)
                bank = (bank_x, bank_p)[p % 2]
                for n, (w, r) in enumerate(parts(mix_hi, mix_lo, x_hi, x_lo)):
                    last = pe.matmul(bank[:, :], w[:, :], r[:, p, :], start=n == 0, stop=n == 2)
                last.then_inc(l0_done, 1)

            def transpose_h(g, par, p):
                pe.wait_ge(h_ready, NP * g + p + 1)
                if p == 0:
                    pe.wait_ge(y_added, NP * g + 3)
                elif isinstance(g, int) and g < 2:
                    pass
                elif p == 2:
                    pe.wait_ge(kt_split, 2 * g - 2)
                else:
                    pe.wait_ge(z_added, NP * g - NP)
                for c in range(DC):
                    s = slice(c * R, (c + 1) * R)
                    last = pe.transpose(hT_banks[p][:, s], h_sb[par][:, p, s], ident[:, :])
                last.then_inc(hT_done, 1)

            def project(g, par, k):
                kind, j = PROJ[k]
                if k == 0:
                    pe.wait_ge(hT_split, NP * g + NP)
                if isinstance(g, int) and g == 0 and k < NRING:
                    pe.wait_ge(setup_split, NSETUP - NRING + 1 + k)
                else:
                    pe.wait_ge(proj_split, NPROJ * g + k - NRING + 1)
                bank = ring[ring_of(k)]
                if kind == "u":
                    s = slice(j * R, (j + 1) * R)
                    terms = [(a[:, i, s], b[:, i, :]) for i in range(DC)
                             for a, b in parts(hT_hi[par], hT_lo[par], M_hi, M_lo)]
                else:
                    terms = [(a[:, ROW_AT[i] + j - i, :], b[:, i, :]) for i in range(j + 1)
                             for a, b in parts(T_hi[kind], T_lo[kind], hT_hi[par], hT_lo[par])]
                for n, (a, b) in enumerate(terms):
                    last = pe.matmul(bank[:, :], a, b, start=n == 0, stop=n == len(terms) - 1)
                last.then_inc(proj_done, 1)

            def gram(g, par, q):
                pe.wait_ge(proj_split, NPROJ * g + 2 * DC)
                if isinstance(g, int) and g == NG - 1:
                    if not q:
                        pe.wait_ge(p_copied, 2 * g)
                elif q:
                    pe.wait_ge(p_copied, 2 * g + q)
                else:
                    pe.wait_ge(y_added, NP * g + 2 * NP)
                for pp in range(2):
                    s = slice((2 * q + pp) * R, (2 * q + pp + 1) * R)
                    terms = [(a[:, i, s], b[:, i, :, s]) for i in range(DC)
                             for a, b in parts(hT_hi[par], hT_lo[par], yT_hi, yT_lo)]
                    for n, (a, b) in enumerate(terms):
                        last = pe.matmul(p_bank(g, q)[:, pp, :, :], a, b, start=n == 0, stop=n == len(terms) - 1)
                last.then_inc(gram_done, 1)

            def transpose_p(g, q):
                d = 2 * g + q
                pe.wait_ge(shift_done, d + 1)
                if q:
                    pe.wait_ge(s2_done, d)
                for pp in range(2):
                    for s in (L, G):
                        last = pe.transpose(pt_ps[:, pp, s, :], P_sb[q][:, pp, s, :], ident[:, :])
                last.then_inc(pt_done, 1)
                pe.wait_ge(cols_ready, d + 1)
                if q:
                    pe.wait_ge(x0_done, d)
                for pp in range(2):
                    last = pe.transpose(row_ps[:, pp, :], inv_norm[q][:, pp:pp + 1].to_broadcast([R, R]), ident[:, :])
                last.then_inc(rows_done, 1)

            def transpose_k(g, q):
                pe.wait_ge(k_done, 2 * g + q + 1)
                if not (isinstance(g, int) and g == NG - 1):
                    pe.wait_ge(s2_done, 2 * g + 2)
                if q:
                    pe.wait_ge(kt_split, 2 * g + 1)
                for pp in range(2):
                    last = pe.transpose(kt_bank(g)[:, pp, :], K_sb[:, pp, :], ident[:, :])
                last.then_inc(kt_done, 1)

            def apply_k(g, p):
                pe.wait_ge(kt_split, 2 * g + p // 2 + 1)
                pe.wait_ge(proj_split, NPROJ * g + 2 * DC + p + 1)
                if p == 1:
                    pe.wait_ge(x0_done, 2 * g + 2)
                elif p >= 2:
                    pe.wait_ge(z_added, NP * g + p - 1)
                bank = (bank_k, bank_r)[p % 2]
                for n, (a, b) in enumerate(parts(KT_hi[p // 2], KT_lo[p // 2], u_hi, u_lo)):
                    last = pe.matmul(bank[:, :], a[:, p % 2, :], b[:, p, :], start=n == 0, stop=n == 2)
                last.then_inc(ku_done, 1)

            def step(g, par, tail=True):
                project(g, par, 0)
                if tail:
                    transpose_p(g - 1, 0)
                project(g, par, 1)
                project(g, par, 2)
                project(g, par, 3)
                if tail:
                    transpose_p(g - 1, 1)
                project(g, par, 4)
                if tail:
                    transpose_k(g - 1, 0)
                project(g, par, 5)
                project(g, par, 6)
                if tail:
                    apply_k(g - 1, 0)
                    apply_k(g - 1, 1)
                project(g, par, 7)
                if tail:
                    transpose_k(g - 1, 1)
                layer0(g + 1, 0)
                layer0(g + 1, 1)
                project(g, par, 8)
                if tail:
                    apply_k(g - 1, 2)
                    apply_k(g - 1, 3)
                layer0(g + 1, 2)
                layer0(g + 1, 3)
                project(g, par, 9)
                project(g, par, 10)
                gram(g, par, 0)
                transpose_h(g + 1, 1 - par, 0)
                transpose_h(g + 1, 1 - par, 1)
                project(g, par, 11)
                transpose_h(g + 1, 1 - par, 2)
                transpose_h(g + 1, 1 - par, 3)
                gram(g, par, 1)

            at = 0

            def setup(cols, terms, split_by=None, split_before=0):
                nonlocal at
                if at >= NRING:
                    pe.wait_ge(setup_split, at - NRING + 1)
                for n, (a, b) in enumerate(terms):
                    if split_by is not None and n % 3 == 0:
                        pe.wait_ge(split_by, split_before + n // 3 + 1)
                    last = pe.matmul(ring[at % NRING][:, 0:cols], a, b, start=n == 0, stop=n == len(terms) - 1)
                last.then_inc(setup_done, 1)
                at += 1

            pe.wait_ge(ident_ready, 2)
            for _ in range(WARM_UP):
                pe.transpose(bank_r[:, 0:R], ident[:, :], ident[:, :])
            pe.wait_ge(mix_steps, 5)
            for s in (L, G):
                layer0(0, 2 * s)
                layer0(0, 2 * s + 1)
                for i in range(DC):
                    setup(D - i * R, [(a[:, e, i * R:(i + 1) * R], b[:, e, i * R:D]) for e in range(DC)
                                      for a, b in parts(W_hi[s], W_lo[s], W_hi[s], W_lo[s])],
                          w_lo_done if i == 0 else None, DC * s)
            pe.wait_ge(w_loaded[3], 16)
            for e in range(DC):
                if e == NRING:
                    transpose_h(0, 0, 0)
                pe.wait_ge(setup_split, at - NRING + 1)
                for f in range(DC):
                    last = pe.transpose(ring[at % NRING][:, f * R:(f + 1) * R],
                                        w_raw[0][:, f, e * R:(e + 1) * R], ident[:, :])
                last.then_inc(setup_done, 1)
                at += 1
            for p in range(1, NP):
                transpose_h(0, 0, p)
            pe.wait_ge(w_lo_done, 3 * DC)
            for i in range(DC):
                setup(D, [(a[:, e, i * R:(i + 1) * R], b[:, e, :]) for e in range(DC)
                          for a, b in parts(W_hi[2], W_lo[2], W_hi[3], W_lo[3])],
                      setup_split if i == 0 else None, 2 * DC)

            step(0, 0, tail=False)
            step(1, 1)
            with pe.Fori(2, NG - 2, 2) as g:
                step(g, 0)
                step(g + 1, 1)
            step(NG - 2, 0)
            g = NG - 1
            project(g, 1, 0)
            transpose_p(g - 1, 0)
            project(g, 1, 1)
            project(g, 1, 2)
            project(g, 1, 3)
            transpose_p(g - 1, 1)
            project(g, 1, 4)
            transpose_k(g - 1, 0)
            project(g, 1, 5)
            project(g, 1, 6)
            apply_k(g - 1, 0)
            transpose_k(g - 1, 1)
            apply_k(g - 1, 1)
            project(g, 1, 7)
            apply_k(g - 1, 2)
            apply_k(g - 1, 3)
            gram(g, 1, 0)
            gram(g, 1, 1)
            pe.wait_ge(kt_split, 2 * g)
            pe.wait_ge(z_added, NP * g)
            transpose_p(g, 0)
            project(g, 1, 8)
            transpose_p(g, 1)
            project(g, 1, 9)
            transpose_k(g, 0)
            project(g, 1, 10)
            apply_k(g, 0)
            apply_k(g, 1)
            transpose_k(g, 1)
            project(g, 1, 11)
            apply_k(g, 2)
            apply_k(g, 3)

        def proj_dst(k, which):
            kind, j = PROJ[k]
            if kind == "u":
                return (u_hi, u_lo)[which][:, j, :]
            return (yT_hi, yT_lo)[which][:, j, kind, :]

        @block.scalar
        def _(act):
            def copy(dst, src, scale=1.0):
                return act.activation(dst, src, ACT.Copy, scale=scale)

            def split_x(g, c):
                if c == 0:
                    act.wait_ge(x_loaded, 16 * g)
                    act.wait_ge(l0_done, NP * g)
                s = slice(2 * c, 2 * c + 2)
                copy(x_hi[:, s, :], x_sb[:, s, :]).then_inc(x_hi_done, 1)

            def split_x0(c):
                act.wait_ge(x0_loaded[c], 16)
                for p in (2 * c, 2 * c + 1):
                    copy(x_hi[:, p, :], x_sb[:, p, :]).then_inc(x0_hi_done, 1)

            def normalise_h(g, par, p):
                act.wait_ge(y_scale, 2 * g + p // 2 + 1)
                act.activation(h_sb[par][:, p, :], h_sb[par][:, p, :], ACT.Identity, scale=y_rs[:, p:p + 1],
                               bias=y_nb[:, p:p + 1]).then_inc(h_ready, 1)

            def hi_hT(g, par, p):
                act.wait_ge(hT_done, NP * g + p + 1)
                copy(hT_hi[par][:, :, p * R:(p + 1) * R],
                     hT_banks[p][:, :].rearrange("p (c r) -> p c r", c=DC)).then_inc(hT_hi_done, 1)

            def hi_proj(g, k):
                act.wait_ge(proj_done, NPROJ * g + k + 1)
                copy(proj_dst(k, 0), ring[ring_of(k)][:, :]).then_inc(proj_hi, 1)

            def copy_p(g, q):
                act.wait_ge(gram_done, 2 * g + q + 1)
                if not (isinstance(g, int) and g == 0):
                    act.wait_ge(s2_done, 2 * g + q - 1)
                copy(P_sb[q][:, :, :, :], p_bank(g, q)).then_inc(p_copied, 1)

            def exp_g(g, q):
                act.wait_ge(s2_done, 2 * g + q + 1)
                act.activation(E_g[:, :, :], S2[:, :, G, :], ACT.Exp, scale=inv_2s2[:, 0:1]).then_inc(exp_done, 1)

            def scale_l(g, q):
                act.wait_ge(coef_done, 2 * g + q + 1)
                for pp in range(2):
                    last = act.activation(K_l[:, pp, :], X_l[:, pp, :], ACT.Copy, scale=coef[:, pp:pp + 1])
                last.then_inc(kl_done, 1)

            def hi_kt(g, q):
                act.wait_ge(kt_done, 2 * g + q + 1)
                copy(KT_hi[q][:, :, :], kt_bank(g)).then_inc(kt_hi_done, 1)

            def normalise_out(g, p):
                act.wait_ge(z_scale, 2 * g + p // 2 + 1)
                act.activation(out_rows(g)[:, p, :], out_rows(g)[:, p, :], ACT.Identity, scale=z_rs[:, p:p + 1],
                               bias=z_nb[:, p:p + 1]).then_inc(o_ready, 1)

            def step(g, par, tail=True):
                split_x(g + 1, 0)
                split_x(g + 1, 1)
                hi_proj(g, 0)
                hi_proj(g, 1)
                if tail:
                    exp_g(g - 1, 0)
                hi_proj(g, 2)
                if tail:
                    scale_l(g - 1, 0)
                hi_proj(g, 3)
                if tail:
                    exp_g(g - 1, 1)
                hi_proj(g, 4)
                if tail:
                    hi_kt(g - 1, 0)
                    scale_l(g - 1, 1)
                hi_proj(g, 5)
                hi_proj(g, 6)
                hi_proj(g, 7)
                if tail:
                    hi_kt(g - 1, 1)
                    normalise_out(g - 1, 0)
                    normalise_out(g - 1, 1)
                hi_proj(g, 8)
                normalise_h(g + 1, 1 - par, 0)
                normalise_h(g + 1, 1 - par, 1)
                if tail:
                    normalise_out(g - 1, 2)
                hi_proj(g, 9)
                if tail:
                    normalise_out(g - 1, 3)
                hi_proj(g, 10)
                copy_p(g, 0)
                normalise_h(g + 1, 1 - par, 2)
                normalise_h(g + 1, 1 - par, 3)
                hi_hT(g + 1, 1 - par, 0)
                hi_hT(g + 1, 1 - par, 1)
                hi_proj(g, 11)
                hi_hT(g + 1, 1 - par, 2)
                hi_hT(g + 1, 1 - par, 3)
                copy_p(g, 1)

            def hi_weight(i):
                act.wait_ge(w_loaded[i], 16)
                for c in range(DC):
                    copy(W_hi[i][:, c, :], w_raw[i][:, c, :]).then_inc(w_hi_done, 1)

            def hi_row(s, i):
                at = DC * s + i
                act.wait_ge(setup_done, at + 1)
                bank = ring[at % NRING]
                last = copy(T_hi[s][:, ROW_AT[i], :], bank[:, 0:R])
                if i < DC - 1:
                    last = copy(T_hi[s][:, ROW_AT[i] + 1:ROW_AT[i] + DC - i, :],
                                bank[:, R:D - i * R].rearrange("p (b c) -> p b c", c=R), scale=2.0)
                last.then_inc(setup_hi, 1)

            split_x0(0)
            hi_weight(0)
            split_x0(1)
            act.wait_ge(gates_loaded, 32)
            act.activation(gate_e[:, 0:1], gates[:, 0:1], ACT.Exp, scale=-1.0)
            act.activation(gate_e[:, 1:2], gates[:, 1:2], ACT.Exp).then_inc(gate_exp, 1)
            hi_row(L, 0)
            hi_weight(1)
            for i in range(1, DC):
                hi_row(L, i)
            normalise_h(0, 0, 0)
            normalise_h(0, 0, 1)
            hi_weight(2)
            for i in range(DC):
                hi_row(G, i)
                if i >= 2:
                    normalise_h(0, 0, i)

            def hi_value(dst, at):
                for i in range(DC):
                    act.wait_ge(setup_done, at + i + 1)
                    copy(dst[:, i, :], ring[(at + i) % NRING][:, :]).then_inc(setup_hi, 1)

            hi_value(W_hi[3], 2 * DC)
            for p in range(NP):
                hi_hT(0, 0, p)
            hi_value(M_hi, 3 * DC)

            step(0, 0, tail=False)
            step(1, 1)
            with act.Fori(2, NG - 2, 2) as g:
                step(g, 0)
                step(g + 1, 1)
            step(NG - 2, 0)
            g = NG - 1
            hi_proj(g, 0)
            hi_proj(g, 1)
            exp_g(g - 1, 0)
            hi_proj(g, 2)
            scale_l(g - 1, 0)
            hi_proj(g, 3)
            exp_g(g - 1, 1)
            hi_proj(g, 4)
            hi_kt(g - 1, 0)
            scale_l(g - 1, 1)
            hi_proj(g, 5)
            hi_proj(g, 6)
            hi_kt(g - 1, 1)
            hi_proj(g, 7)
            copy_p(g, 0)
            normalise_out(g - 1, 0)
            copy_p(g, 1)
            normalise_out(g - 1, 1)
            exp_g(g, 0)
            hi_proj(g, 8)
            scale_l(g, 0)
            exp_g(g, 1)
            hi_kt(g, 0)
            hi_proj(g, 9)
            scale_l(g, 1)
            hi_kt(g, 1)
            hi_proj(g, 10)
            hi_proj(g, 11)
            normalise_out(g - 1, 2)
            normalise_out(g - 1, 3)
            for p in range(NP - 1):
                normalise_out(g, p)

        @block.vector
        def _(dve):
            def add_y(g, par, q):
                for p in (2 * q, 2 * q + 1):
                    dve.wait_ge(l0_done, NP * g + p + 1)
                    dve.tensor_tensor(h_sb[par][:, p, :], (bank_x, bank_p)[p % 2][:, :], bias_bc[:, :],
                                      ALU.add).then_inc(y_added, 1)

            def count_y(g, par, q):
                duo = (2 * q, 2 * q + 1)
                for p in duo:
                    dve.wait_ge(y_added, NP * g + p + 1)
                    dve.bn_stats(y_bn[:, p, :], h_sb[par][:, p, :]).then_inc(y_counted, 1)
                dve.wait_ge(y_counted, NP * g + 2 * q + 2)
                settle(dve)
                for p in duo:
                    last = dve.bn_aggr(y_mv[:, p, :], y_bn[:, p, :])
                last.then_inc(y_stats, 1)

            def lo_hT(g, par, p):
                dve.wait_ge(hT_hi_done, NP * g + p + 1)
                s = slice(p * R, (p + 1) * R)
                dve.tensor_tensor(hT_lo[par][:, :, s], hT_banks[p][:, :].rearrange("p (c r) -> p c r", c=DC),
                                  hT_hi[par][:, :, s], ALU.subtract).then_inc(hT_split, 1)

            def lo_proj(g, k):
                dve.wait_ge(proj_hi, NPROJ * g + k + 1)
                dve.tensor_tensor(proj_dst(k, 1), ring[ring_of(k)][:, :], proj_dst(k, 0),
                                  ALU.subtract).then_inc(proj_split, 1)

            def diagonals(g, q):
                dve.wait_ge(p_copied, 2 * g + q + 1)
                if q:
                    dve.wait_ge(sq_done, 2 * g + q)
                for pp in range(2):
                    for s in (L, G):
                        last = dve.tensor_tensor_reduce(
                            out=diag_scr[:, 2 * pp + s, :], in0=P_sb[q][:, pp, s, :], in1=ident[:, :], scale=1.0,
                            scalar=0.0, op0=ALU.mult, op1=ALU.add, accum_out=sq[q][:, s, pp:pp + 1])
                last.then_inc(sq_done, 1)
                dve.wait_ge(sq_done, 2 * g + q + 1)
                settle(dve)
                for pp in range(2):
                    last = dve.tensor_scalar(P_sb[q][:, pp, G, :], P_sb[q][:, pp, G, :], sq[q][:, G, pp:pp + 1], None,
                                             ALU.subtract)
                last.then_inc(shift_done, 1)

            def similarities(g, q):
                add_p(g, q)
                weigh(g, q)

            def add_p(g, q):
                d = 2 * g + q
                dve.wait_ge(pt_done, d + 1)
                dve.tensor_tensor(S2[:, :, :, :], pt_ps, P_sb[q][:, :, :, :], ALU.add).then_inc(s2_done, 1)

            def weigh(g, q):
                d = 2 * g + q
                dve.wait_ge(rows_done, d + 1)
                dve.wait_ge(s2_done, d + 1)
                dve.scalar_tensor_tensor(X0[:, :, :], S2[:, :, L, :], 0.0, row_ps, ALU.max,
                                         ALU.mult).then_inc(x0_done, 1)
                dve.wait_ge(x0_done, d + 1)
                for pp in range(2):
                    last = dve.tensor_tensor_reduce(
                        out=X_l[:, pp, :], in0=X0[:, pp, :], in1=mask[:, :], scale=1.0, scalar=0.0,
                        op0=ALU.mult, op1=ALU.add, accum_out=sums[:, pp:pp + 1])
                last.then_inc(xl_done, 1)

            def coefficients(g, q):
                d = 2 * g + q
                dve.wait_ge(exp_done, d + 1)
                for pp in range(2):
                    last = dve.scalar_tensor_tensor(X_g[:, pp, :], E_g[:, pp, :], 1.0, mask[:, :], ALU.min, ALU.mult,
                                                    accum_out=sums[:, 2 + pp:3 + pp])
                last.then_inc(xg_done, 1)
                dve.wait_ge(xg_done, d + 1)
                dve.wait_ge(xl_done, d + 1)
                dve.wait_ge(floors_ready, d + 1)
                dve.tensor_tensor(dens[:, :], sums[:, :], floors[q][:, :], ALU.max).then_inc(dens_done, 1)
                dve.wait_ge(dens_done, d + 1)
                dve.reciprocal(recs[:, :], dens[:, :]).then_inc(recs_done, 1)
                dve.wait_ge(recs_done, d + 1)
                dve.tensor_tensor(coef[:, :], recs[:, :], mixw[:, :], ALU.mult).then_inc(coef_done, 1)

            def combine(g, q):
                dve.wait_ge(coef_done, 2 * g + q + 1)
                dve.wait_ge(kl_done, 2 * g + q + 1)
                for pp in range(2):
                    last = dve.scalar_tensor_tensor(K_sb[:, pp, :], X_g[:, pp, :], coef[:, 2 + pp:3 + pp],
                                                    K_l[:, pp, :], ALU.mult, ALU.add)
                last.then_inc(k_done, 1)

            def lo_kt(g, q):
                dve.wait_ge(kt_hi_done, 2 * g + q + 1)
                dve.tensor_tensor(KT_lo[q][:, :, :], kt_bank(g), KT_hi[q][:, :, :], ALU.subtract).then_inc(kt_split, 1)

            def add_z_pair(g, par, p):
                dve.wait_ge(ku_done, NP * g + p + 1)
                if not (isinstance(g, int) and g in (0, NG - 1)):
                    dve.wait_ge(stored[p], 16 * g)
                dve.tensor_tensor(out_rows(g)[:, p, :], (bank_k, bank_r)[p % 2][:, :], h_sb[par][:, p, :],
                                  ALU.add).then_inc(z_added, 1)

            def count_z_pair(g, p):
                dve.wait_ge(z_added, NP * g + p + 1)
                dve.bn_stats(z_bn[:, p, :], out_rows(g)[:, p, :]).then_inc(z_counted, 1)

            def gather_z(g, q):
                dve.wait_ge(z_counted, NP * g + 2 * q + 2)
                if isinstance(g, int) and g == NG - 1:
                    dve.wait_ge(z_scale, 2 * g - 1 + q)
                settle(dve)
                for p in (2 * q, 2 * q + 1):
                    last = dve.bn_aggr(z_mv[:, p, :], z_bn[:, p, :])
                last.then_inc(z_stats, 1)

            def add_z(g, par, q):
                for p in (2 * q, 2 * q + 1):
                    add_z_pair(g, par, p)

            def count_z(g, q):
                for p in (2 * q, 2 * q + 1):
                    count_z_pair(g, p)
                gather_z(g, q)

            def step(g, par, tail=True):
                if tail:
                    diagonals(g - 1, 1)
                lo_proj(g, 0)
                if tail:
                    similarities(g - 1, 0)
                lo_proj(g, 1)
                if tail:
                    coefficients(g - 1, 0)
                lo_proj(g, 2)
                if tail:
                    combine(g - 1, 0)
                lo_proj(g, 3)
                if tail:
                    similarities(g - 1, 1)
                    coefficients(g - 1, 1)
                    lo_kt(g - 1, 0)
                lo_proj(g, 4)
                if tail:
                    combine(g - 1, 1)
                lo_proj(g, 5)
                lo_proj(g, 6)
                if tail:
                    add_z(g - 1, 1 - par, 0)
                    count_z(g - 1, 0)
                lo_proj(g, 7)
                if tail:
                    lo_kt(g - 1, 1)
                add_y(g + 1, 1 - par, 0)
                count_y(g + 1, 1 - par, 0)
                lo_proj(g, 8)
                if tail:
                    add_z(g - 1, 1 - par, 1)
                    count_z(g - 1, 1)
                add_y(g + 1, 1 - par, 1)
                count_y(g + 1, 1 - par, 1)
                lo_proj(g, 9)
                lo_proj(g, 10)
                diagonals(g, 0)
                lo_hT(g + 1, 1 - par, 0)
                lo_hT(g + 1, 1 - par, 1)
                lo_proj(g, 11)
                lo_hT(g + 1, 1 - par, 2)
                lo_hT(g + 1, 1 - par, 3)

            dve.wait_ge(ident_ready, 2)
            dve.tensor_scalar(off_diag[:, :], ident[:, :], -1.0, 1.0, ALU.mult, ALU.add).then_inc(mix_steps, 1)
            dve.wait_ge(adj_loaded, 32)
            dve.tensor_tensor(mix[:, :], adj_bd[:, :], adj_bd[:, :], ALU.mult).then_inc(mix_steps, 1)
            dve.wait_ge(mix_steps, 2)
            dve.tensor_tensor(mix[:, :], mix[:, :], ident[:, :], ALU.add).then_inc(mix_steps, 1)
            dve.wait_ge(mix_steps, 3)
            dve.tensor_copy(mix_hi[:, :], mix[:, :]).then_inc(mix_steps, 1)
            dve.wait_ge(mix_steps, 4)
            dve.tensor_tensor(mix_lo[:, :], mix[:, :], mix_hi[:, :], ALU.subtract).then_inc(mix_steps, 1)

            def lo_weight(i, first, end):
                for c in range(first, end):
                    dve.wait_ge(w_hi_done, DC * i + c + 1)
                    dve.tensor_tensor(W_lo[i][:, c, :], w_raw[i][:, c, :], W_hi[i][:, c, :],
                                      ALU.subtract).then_inc(w_lo_done, 1)

            def lo_row(s, i):
                at = DC * s + i
                dve.wait_ge(setup_hi, at + 1)
                bank = ring[at % NRING]
                first = ROW_AT[i]
                last = dve.tensor_tensor(T_lo[s][:, first, :], bank[:, 0:R], T_hi[s][:, first, :], ALU.subtract)
                if i < DC - 1:
                    b = slice(first + 1, first + DC - i)
                    last = dve.scalar_tensor_tensor(
                        T_lo[s][:, b, :], bank[:, R:D - i * R].rearrange("p (b c) -> p b c", c=R), 2.0,
                        T_hi[s][:, b, :], ALU.mult, ALU.subtract)
                last.then_inc(setup_split, 1)

            def split_x0(c):
                for p in (2 * c, 2 * c + 1):
                    dve.wait_ge(x0_hi_done, p + 1)
                    dve.tensor_tensor(x_lo[:, p, :], x_sb[:, p, :], x_hi[:, p, :], ALU.subtract).then_inc(x_lo_done, 1)

            split_x0(0)
            dve.tensor_tensor(mask[:, :], adj_bd[:, :], off_diag[:, :], ALU.mult).then_inc(mix_steps, 1)
            lo_weight(0, 0, DC)
            split_x0(1)
            dve.wait_ge(bias_loaded, 16)
            add_y(0, 0, 0)
            lo_row(L, 0)
            count_y(0, 0, 0)
            lo_weight(1, 0, 2)
            lo_row(L, 1)
            lo_weight(1, 2, DC)
            lo_row(L, 2)
            lo_row(L, 3)
            dve.wait_ge(gate_exp, 1)
            dve.tensor_scalar(gate_t[:, 0:1], gate_e[:, 0:1], 1.0, None, ALU.add)
            dve.scalar_tensor_tensor(gate_t[:, 1:2], gate_e[:, 1:2], 2.0, gate_e[:, 1:2], ALU.mult,
                                     ALU.mult).then_inc(gate_steps, 1)
            dve.wait_ge(gate_steps, 1)
            dve.reciprocal(gate_t[:, 2:4], gate_t[:, 0:2]).then_inc(gate_steps, 1)
            dve.wait_ge(gate_steps, 2)
            dve.tensor_copy(inv_2s2[:, :], gate_t[:, 3:4])
            dve.tensor_copy(mixw[:, 0:2], gate_t[:, 2:3].to_broadcast([R, 2]))
            dve.tensor_scalar(mixw[:, 2:4], gate_t[:, 2:3].to_broadcast([R, 2]), -1.0, 1.0, ALU.mult,
                              ALU.add).then_inc(gate_steps, 1)
            dve.wait_ge(gate_steps, 3)
            add_y(0, 0, 1)
            count_y(0, 0, 1)
            for i in range(DC):
                lo_row(G, i)
                lo_weight(2, i, i + 1)

            def lo_value(hi, lo, at):
                for i in range(DC):
                    dve.wait_ge(setup_hi, at + i + 1)
                    dve.tensor_tensor(lo[:, i, :], ring[(at + i) % NRING][:, :], hi[:, i, :],
                                      ALU.subtract).then_inc(setup_split, 1)

            lo_value(W_hi[3], W_lo[3], 2 * DC)
            for p in range(NP):
                lo_hT(0, 0, p)
            lo_value(M_hi, M_lo, 3 * DC)

            step(0, 0, tail=False)
            step(1, 1)
            with dve.Fori(2, NG - 2, 2) as g:
                step(g, 0)
                step(g + 1, 1)
            step(NG - 2, 0)
            g = NG - 1
            diagonals(g - 1, 1)
            lo_proj(g, 0)
            similarities(g - 1, 0)
            lo_proj(g, 1)
            coefficients(g - 1, 0)
            lo_proj(g, 2)
            combine(g - 1, 0)
            lo_proj(g, 3)
            similarities(g - 1, 1)
            coefficients(g - 1, 1)
            lo_kt(g - 1, 0)
            lo_proj(g, 4)
            combine(g - 1, 1)
            lo_proj(g, 5)
            lo_proj(g, 6)
            lo_kt(g - 1, 1)
            add_z(g - 1, 0, 0)
            lo_proj(g, 7)
            add_z(g - 1, 0, 1)
            count_z(g - 1, 0)
            diagonals(g, 0)
            count_z_pair(g - 1, 2)
            add_p(g, 0)
            diagonals(g, 1)
            weigh(g, 0)
            coefficients(g, 0)
            add_p(g, 1)
            combine(g, 0)
            weigh(g, 1)
            lo_proj(g, 8)
            lo_kt(g, 0)
            coefficients(g, 1)
            lo_proj(g, 9)
            combine(g, 1)
            count_z_pair(g - 1, 3)
            gather_z(g - 1, 1)
            lo_kt(g, 1)
            lo_proj(g, 10)
            add_z(g, 1, 0)
            count_z_pair(g, 0)
            lo_proj(g, 11)
            add_z_pair(g, 1, 2)
            count_z_pair(g, 1)
            gather_z(g, 0)
            add_z_pair(g, 1, 3)
            count_z_pair(g, 2)
            count_z_pair(g, 3)
            gather_z(g, 1)
            dve.wait_ge(z_scale, 2 * g + 2)
            settle(dve)
            last_rows = out_rows(g)[:, NP - 1, :]
            dve.tensor_scalar(last_rows, last_rows, z_rs[:, NP - 1:NP], z_nb[:, NP - 1:NP], ALU.mult,
                              ALU.add).then_inc(o_last_ready, 1)

        @block.gpsimd
        def _(pool):
            def split_x(g, p):
                pool.wait_ge(x_hi_done, 2 * g + p // 2 - 1)
                pool.tensor_tensor(x_lo[:, p, :], x_sb[:, p, :], x_hi[:, p, :], ALU.subtract).then_inc(x_lo_done, 1)

            def scale_of(stats, ve_done, rs_done, scale, mv, ve, nm, rs, nb, d, q):
                pq = slice(2 * q, 2 * q + 2)
                pool.wait_ge(stats, d + 1)
                settle(pool)
                pool.tensor_scalar(ve[:, pq], mv[:, pq, 1], LN_EPS, None, ALU.add).then_inc(ve_done, 1)
                pool.wait_ge(ve_done, d + 1)
                pool.tensor_tensor(rs[:, pq], ve[:, pq], pow_neg_half[:, :], ALU.pow).then_inc(rs_done, 1)
                pool.tensor_scalar(nm[:, pq], mv[:, pq, 0], -1.0, None, ALU.mult).then_inc(rs_done, 1)
                pool.wait_ge(rs_done, 2 * d + 2)
                pool.tensor_tensor(nb[:, pq], nm[:, pq], rs[:, pq], ALU.mult).then_inc(scale, 1)

            def scale_y(g, q):
                scale_of(y_stats, y_ve_done, y_rs_done, y_scale, y_mv, y_ve, y_nm, y_rs, y_nb, 2 * g + q, q)

            def scale_z(g, q):
                scale_of(z_stats, z_ve_done, z_rs_done, z_scale, z_mv, z_ve, z_nm, z_rs, z_nb, 2 * g + q, q)

            def columns(g, q):
                d = 2 * g + q
                pool.wait_ge(sq_done, d + 1)
                settle(pool)
                pool.tensor_scalar(sq_floor[q][:, :], sq[q][:, L, :], EPS * EPS, None, ALU.max).then_inc(floor_done, 1)
                pool.wait_ge(floor_done, d + 1)
                pool.tensor_tensor(inv_norm[q][:, :], sq_floor[q][:, :], pow_neg_half[:, :],
                                   ALU.pow).then_inc(cols_ready, 1)
                pool.tensor_scalar(sq_eps[q][:, :], sq_floor[q][:, :], 2 * EPS, None, ALU.mult).then_inc(sq_eps_done, 1)
                pool.wait_ge(cols_ready, d + 1)
                pool.wait_ge(sq_eps_done, d + 1)
                pool.tensor_tensor(floors[q][:, 0:2], sq_eps[q][:, :], inv_norm[q][:, :],
                                   ALU.mult).then_inc(floors_ready, 1)

            def step(g, tail=True):
                if tail:
                    columns(g - 1, 1)
                for p in range(NP):
                    split_x(g + 1, p)
                for q in range(2):
                    if tail:
                        scale_z(g - 1, q)
                    scale_y(g + 1, q)
                columns(g, 0)

            pool.memset(adj_bd[:, :], 0.0).then_inc(adj_zeroed, 1)
            pool.memset(ident[:, :], 0.0).then_inc(ident_ready, 1)
            pool.wait_ge(ident_ready, 1)
            pool.affine_select(out=ident[:, :], in_=ident[:, :], compare_op=ALU.not_equal, fill=1.0, base=0,
                               pattern=[[-1, R]], channel_multiplier=1).then_inc(ident_ready, 1)
            pool.memset(pow_neg_half[:, :], -0.5)
            pool.memset(floors[0][:, 2:4], EPS)
            pool.memset(floors[1][:, 2:4], EPS).then_inc(pow_ready, 1)
            pool.wait_ge(pow_ready, 1)
            for q in range(2):
                scale_y(0, q)

            step(0, tail=False)
            step(1)
            with pool.Fori(2, NG - 2, 1) as g:
                step(g)
            step(NG - 2)
            g = NG - 1
            columns(g - 1, 1)
            scale_z(g - 1, 0)
            columns(g, 0)
            columns(g, 1)
            scale_z(g - 1, 1)
            for q in range(2):
                pool.wait_ge(o_ready, NP * (g - 1) + 2 * q + 2)
                scale_z(g, q)


_INS = ['x', 'adj', 'L0_gnn_bias', 'L1_gnn_W_lang', 'L1_gnn_W_grav', 'L1_gnn_W_V', 'L1_gnn_W_O', 'L1_gnn_gate_logit',
        'L1_gnn_log_sigma']
_OUTS = [((128, 64, 512), 'float32')]


def kernel(**inputs):
    import numpy as _np
    import concourse.bacc as _bacc
    from concourse import mybir as _mybir
    from concourse.bass_utils import run_bass_kernel_spmd as _run

    nc = _bacc.Bacc("TRN2", target_bir_lowering=False, num_devices=1)
    arrays, args = {}, []
    for name in _INS:
        a = _np.ascontiguousarray(inputs[name])
        arrays[f"in_{name}_dram"] = a
        args.append(nc.dram_tensor(f"in_{name}_dram", a.shape, _mybir.dt.from_np(a.dtype), kind="ExternalInput").ap())
    for i, (shape, dtype) in enumerate(_OUTS):
        dt = _mybir.dt.from_np(_np.dtype(dtype))
        args.append(nc.dram_tensor(f"out_{i}_dram", shape, dt, kind="ExternalOutput").ap())
    bass_two_layer_graph_resnorm(nc, *args)
    r = _run(nc, [arrays], core_ids=[0])
    got = tuple(r.results[0][f"out_{i}_dram"] for i in range(len(_OUTS)))
    return got[0]
```
